# Optimizing a Trainium2 kernel written in Bass

```python
import numpy as np
import jax
import jax.numpy as jnp

def _softmax(x, axis=-1):
    return jax.nn.softmax(x, axis=axis)

def _gelu(x):
    return jax.nn.gelu(x, approximate=True)

def _silu(x):
    return jax.nn.silu(x)

def _sigmoid(x):
    return jax.nn.sigmoid(x)

def _layernorm(x, axis=-1, eps=1e-05):
    m = jnp.mean(x, axis=axis, keepdims=True)
    v = jnp.var(x, axis=axis, keepdims=True)
    return (x - m) / jnp.sqrt(v + eps)

def _scatter_add(tgt, idx, src, axis=0):
    return tgt.at[idx].add(src)

def _segment_sum(src, seg, n):
    return jax.ops.segment_sum(src, seg, n)
kernel_name = 'mk_adj_resnorm_d4_adj_r2_53b48c'

def setup_inputs(seed: int=0):
    np.random.seed(seed)
    _w = jnp.asarray

    def _rec_inputs():
        import jax
        import jax.numpy as jnp
        _gk = jax.random.key(seed)
        x = -0.000929 + 1 * jax.random.normal(jax.random.fold_in(_gk, 1), (8, 1024, 128), jnp.float32)
        _w = (1.0 + jnp.arange(1024, dtype=jnp.float32)) ** (-0.5)
        _w = _w / _w.mean()
        _pij = jnp.clip(0.0078125 * _w[:, None] * _w[None, :], 0.0, 1.0)
        _a = jax.random.uniform(jax.random.fold_in(_gk, 2), (1024, 1024)) < _pij
        _a = jnp.logical_or(_a, jnp.eye(1024, dtype=bool))
        adj = _a.astype(jnp.int32)
        return (x, adj)
    x, adj = _rec_inputs()

    def _L0_gnn_setup():
        import jax, jax.numpy as jnp
        import numpy as np
        ALPHA = 0.2
        EPS = 1e-06
        key = jax.random.key(seed)
        ks = jax.random.split(key, 8)
        B, N, D, H = (2, 1024, 128, 8)
        dh = D // H
        x = jax.random.normal(ks[0], (B, N, D), dtype=jnp.float32)
        adj = jax.random.randint(ks[1], (N, N), 0, 2, dtype=jnp.int32)
        adj = jnp.maximum(adj, jnp.eye(N, dtype=jnp.int32))
        p = jax.random.uniform(ks[2], (B, N, N), dtype=jnp.float32)
        prior = p / jnp.sum(p, axis=-1, keepdims=True)
        W = jax.random.normal(ks[3], (H, D, dh), dtype=jnp.float32) * (1.0 / np.sqrt(D))
        a_src = jax.random.normal(ks[4], (H, dh), dtype=jnp.float32) * (1.0 / np.sqrt(dh))
        a_dst = jax.random.normal(ks[5], (H, dh), dtype=jnp.float32) * (1.0 / np.sqrt(dh))
        beta_tilde = jnp.ones((), dtype=jnp.float32)
        W_out = jax.random.normal(ks[6], (D, D), dtype=jnp.float32) * (1.0 / np.sqrt(D))
        return {'x': x, 'adj': adj, 'prior': prior, 'W': W, 'a_src': a_src, 'a_dst': a_dst, 'beta_tilde': beta_tilde, 'W_out': W_out}
    _L0_gnn_all = _L0_gnn_setup()
    _L0_gnn_in = {k: v for k, v in _L0_gnn_all.items() if k in ('W', 'a_src', 'a_dst', 'beta_tilde', 'W_out')}
    del _L0_gnn_all

    def _L1_gnn_setup():
        import jax, jax.numpy as jnp
        import numpy as np
        IN_F = 128
        OUT_F = 128
        ALPHA = 0.01
        NEG_INF = -1000000000.0
        key = jax.random.key(seed)
        k_inp, k_adj, k_W, k_a = jax.random.split(key, 4)
        inp = jax.random.normal(k_inp, (8, 1024, IN_F), dtype=jnp.float32)
        adj = jax.random.randint(k_adj, (1024, 1024), 0, 2, dtype=jnp.int32)
        gain = 1.414
        lim_W = gain * np.sqrt(6.0 / (IN_F + OUT_F))
        W = jax.random.uniform(k_W, (IN_F, OUT_F), minval=-lim_W, maxval=lim_W, dtype=jnp.float32)
        lim_a = gain * np.sqrt(6.0 / (2 * OUT_F + 1))
        a = jax.random.uniform(k_a, (2 * OUT_F, 1), minval=-lim_a, maxval=lim_a, dtype=jnp.float32)
        return {'inp': inp, 'adj': adj, 'W': W, 'a': a}
    _L1_gnn_all = _L1_gnn_setup()
    _L1_gnn_in = {k: v for k, v in _L1_gnn_all.items() if k in ('W', 'a')}
    del _L1_gnn_all

    def _L2_gnn_setup():
        import jax, jax.numpy as jnp
        import numpy as np
        import math
        CHUNK = 128
        NUM_HEADS = 4
        EPS = 1e-05
        key = jax.random.key(seed)
        ks = jax.random.split(key, 12)
        B, N, F = (4, 1024, 128)
        x = jax.random.normal(ks[0], (B, N, F), dtype=jnp.float32)
        adj_matrix = jax.random.randint(ks[1], (N, N), 0, 2, dtype=jnp.int32)
        s = 1.0 / math.sqrt(F)
        Wq = jax.random.normal(ks[2], (F, F), dtype=jnp.float32) * s
        bq = jnp.zeros((F,), dtype=jnp.float32)
        Wk = jax.random.normal(ks[3], (F, F), dtype=jnp.float32) * s
        bk = jnp.zeros((F,), dtype=jnp.float32)
        Wv = jax.random.normal(ks[4], (F, F), dtype=jnp.float32) * s
        bv = jnp.zeros((F,), dtype=jnp.float32)
        Wo = jax.random.normal(ks[5], (F, F), dtype=jnp.float32) * s
        bo = jnp.zeros((F,), dtype=jnp.float32)
        gamma = jnp.ones((F,), dtype=jnp.float32)
        beta = jnp.zeros((F,), dtype=jnp.float32)
        return {'x': x, 'adj_matrix': adj_matrix, 'Wq': Wq, 'bq': bq, 'Wk': Wk, 'bk': bk, 'Wv': Wv, 'bv': bv, 'Wo': Wo, 'bo': bo, 'gamma': gamma, 'beta': beta}
    _L2_gnn_all = _L2_gnn_setup()
    _L2_gnn_in = {k: v for k, v in _L2_gnn_all.items() if k in ('Wq', 'bq', 'Wk', 'bk', 'Wv', 'bv', 'Wo', 'bo', 'gamma', 'beta')}
    del _L2_gnn_all

    def _L3_gnn_setup():
        import jax, jax.numpy as jnp
        import numpy as np
        B, N, D_IN, D_OUT, H = (64, 256, 128, 128, 4)
        HD = D_OUT // H
        key = jax.random.key(seed)
        ks = jax.random.split(key, 10)
        x = jax.random.normal(ks[0], (B, N, D_IN), dtype=jnp.float32)
        adj = jax.random.randint(ks[1], (N, N), 0, 2, dtype=jnp.int32)
        adj = adj.at[jnp.arange(N), jnp.arange(N)].set(1)
        s_in = 1.0 / np.sqrt(D_IN)
        s_out = 1.0 / np.sqrt(D_OUT)
        wq = jax.random.uniform(ks[2], (D_OUT, D_IN), jnp.float32, -s_in, s_in)
        bq = jax.random.uniform(ks[3], (D_OUT,), jnp.float32, -s_in, s_in)
        wk = jax.random.uniform(ks[4], (D_OUT, D_IN), jnp.float32, -s_in, s_in)
        bk = jax.random.uniform(ks[5], (D_OUT,), jnp.float32, -s_in, s_in)
        wv = jax.random.uniform(ks[6], (D_OUT, D_IN), jnp.float32, -s_in, s_in)
        bv = jax.random.uniform(ks[7], (D_OUT,), jnp.float32, -s_in, s_in)
        wo = jax.random.uniform(ks[8], (D_OUT, D_OUT), jnp.float32, -s_out, s_out)
        bo = jax.random.uniform(ks[9], (D_OUT,), jnp.float32, -s_out, s_out)
        return {'x': x, 'adj': adj, 'wq': wq, 'bq': bq, 'wk': wk, 'bk': bk, 'wv': wv, 'bv': bv, 'wo': wo, 'bo': bo}
    _L3_gnn_all = _L3_gnn_setup()
    _L3_gnn_in = {k: v for k, v in _L3_gnn_all.items() if k in ('wq', 'bq', 'wk', 'bk', 'wv', 'bv', 'wo', 'bo')}
    del _L3_gnn_all
    return {'x': x, 'adj': adj, 'L0_gnn_W': _L0_gnn_in['W'], 'L0_gnn_a_src': _L0_gnn_in['a_src'], 'L0_gnn_a_dst': _L0_gnn_in['a_dst'], 'L0_gnn_beta_tilde': _L0_gnn_in['beta_tilde'], 'L0_gnn_W_out': _L0_gnn_in['W_out'], 'L1_gnn_W': _L1_gnn_in['W'], 'L1_gnn_a': _L1_gnn_in['a'], 'L2_gnn_Wq': _L2_gnn_in['Wq'], 'L2_gnn_bq': _L2_gnn_in['bq'], 'L2_gnn_Wk': _L2_gnn_in['Wk'], 'L2_gnn_bk': _L2_gnn_in['bk'], 'L2_gnn_Wv': _L2_gnn_in['Wv'], 'L2_gnn_bv': _L2_gnn_in['bv'], 'L2_gnn_Wo': _L2_gnn_in['Wo'], 'L2_gnn_bo': _L2_gnn_in['bo'], 'L2_gnn_gamma': _L2_gnn_in['gamma'], 'L2_gnn_beta': _L2_gnn_in['beta'], 'L3_gnn_wq': _L3_gnn_in['wq'], 'L3_gnn_bq': _L3_gnn_in['bq'], 'L3_gnn_wk': _L3_gnn_in['wk'], 'L3_gnn_bk': _L3_gnn_in['bk'], 'L3_gnn_wv': _L3_gnn_in['wv'], 'L3_gnn_bv': _L3_gnn_in['bv'], 'L3_gnn_wo': _L3_gnn_in['wo'], 'L3_gnn_bo': _L3_gnn_in['bo']}

def reference(x, adj, L0_gnn_W, L0_gnn_a_src, L0_gnn_a_dst, L0_gnn_beta_tilde, L0_gnn_W_out, L1_gnn_W, L1_gnn_a, L2_gnn_Wq, L2_gnn_bq, L2_gnn_Wk, L2_gnn_bk, L2_gnn_Wv, L2_gnn_bv, L2_gnn_Wo, L2_gnn_bo, L2_gnn_gamma, L2_gnn_beta, L3_gnn_wq, L3_gnn_bq, L3_gnn_wk, L3_gnn_bk, L3_gnn_wv, L3_gnn_bv, L3_gnn_wo, L3_gnn_bo):
    import jax
    import jax.numpy as jnp

    def _L0_gnn_ref(x, adj, prior, W, a_src, a_dst, beta_tilde, W_out):
        import jax, jax.numpy as jnp
        import numpy as np
        ALPHA = 0.2
        EPS = 1e-06
        B, N, D = x.shape
        x_proj = jnp.einsum('bnd,hdf->bhnf', x, W)
        e_src = jnp.einsum('bhnf,hf->bhn', x_proj, a_src)
        e_dst = jnp.einsum('bhnf,hf->bhn', x_proj, a_dst)
        e = jax.nn.leaky_relu(e_src[..., :, None] + e_dst[..., None, :], ALPHA)
        beta = jax.nn.softplus(beta_tilde)
        e = e + (beta * jnp.log(prior + EPS))[:, None, :, :]
        neg_inf = jnp.finfo(e.dtype).min
        e = jnp.where(adj[None, None, :, :] > 0, e, neg_inf)
        attn = jax.nn.softmax(e, axis=-1)
        h = jnp.einsum('bhij,bhjf->bhif', attn, x_proj)
        h = h.transpose(0, 2, 1, 3).reshape(B, N, D)
        return h @ W_out.T

    def _L1_gnn_ref(inp, adj, W, a):
        import jax, jax.numpy as jnp
        import numpy as np
        IN_F = 128
        OUT_F = 128
        ALPHA = 0.01
        NEG_INF = -1000000000.0
        h = jnp.matmul(inp, W)
        a1 = a[:OUT_F, 0]
        a2 = a[OUT_F:, 0]
        e_src = jnp.einsum('bnf,f->bn', h, a1)
        e_dst = jnp.einsum('bnf,f->bn', h, a2)
        e = jax.nn.leaky_relu(e_src[:, :, None] + e_dst[:, None, :], negative_slope=ALPHA)
        e = jnp.where(adj[None, :, :] == 0, NEG_INF, e)
        attention = jax.nn.softmax(e, axis=-1)
        h_prime = jnp.matmul(attention, h)
        return jax.nn.relu(h_prime)

    def _L2_gnn_ref(x, adj_matrix, Wq, bq, Wk, bk, Wv, bv, Wo, bo, gamma, beta):
        import jax, jax.numpy as jnp
        import numpy as np
        import math
        CHUNK = 128
        NUM_HEADS = 4
        EPS = 1e-05
        B, N, Fin = x.shape
        H = NUM_HEADS
        Dout = Wq.shape[0]
        Dh = Dout // H
        Nc = N // CHUNK
        q = (x @ Wq.T + bq).reshape(B, N, H, Dh).transpose(0, 2, 1, 3)
        k = (x @ Wk.T + bk).reshape(B, N, H, Dh).transpose(0, 2, 1, 3)
        v = (x @ Wv.T + bv).reshape(B, N, H, Dh).transpose(0, 2, 1, 3)
        kc = k.reshape(B, H, Nc, CHUNK, Dh)
        vc = v.reshape(B, H, Nc, CHUNK, Dh)
        scores = jnp.einsum('bhnd,bhjcd->bhnjc', q, kc) / jnp.sqrt(jnp.asarray(Dh, dtype=q.dtype))
        scores = jnp.clip(scores, -10.0, 10.0)
        mask = adj_matrix.reshape(N, Nc, CHUNK)[None, None]
        scores = jnp.where(mask == 0, jnp.asarray(-10.0, scores.dtype), scores)
        attn = jax.nn.softmax(scores, axis=-1)
        ctx = jnp.einsum('bhnjc,bhjcd->bhnd', attn, vc)
        ctx = ctx.transpose(0, 2, 1, 3).reshape(B, N, Dout)
        out = ctx @ Wo.T + bo
        out = out + x
        mu = jnp.mean(out, axis=-1, keepdims=True)
        var = jnp.mean(jnp.square(out - mu), axis=-1, keepdims=True)
        out = (out - mu) * jax.lax.rsqrt(var + EPS) * gamma + beta
        return out

    def _L3_gnn_ref(x, adj, wq, bq, wk, bk, wv, bv, wo, bo):
        import jax, jax.numpy as jnp
        import numpy as np
        B, N, D_IN, D_OUT, H = (64, 256, 128, 128, 4)
        HD = D_OUT // H
        b, n, _ = x.shape
        q = (x @ wq.T + bq).reshape(b, n, H, HD).transpose(0, 2, 1, 3)
        k = (x @ wk.T + bk).reshape(b, n, H, HD).transpose(0, 2, 1, 3)
        v = (x @ wv.T + bv).reshape(b, n, H, HD).transpose(0, 2, 1, 3)
        scores = jnp.einsum('bhnd,bhmd->bhnm', q, k) / jnp.sqrt(jnp.float32(HD))
        scores = jnp.where(adj[None, None] == 0, -jnp.inf, scores)
        attn = jnp.nan_to_num(jax.nn.softmax(scores, axis=-1), nan=0.0)
        out = jnp.einsum('bhnm,bhmd->bhnd', attn, v)
        out = out.transpose(0, 2, 1, 3).reshape(b, n, D_OUT)
        return out @ wo.T + bo
    x = _layernorm(x + _L0_gnn_ref(x, adj, adj[None], L0_gnn_W, L0_gnn_a_src, L0_gnn_a_dst, L0_gnn_beta_tilde, L0_gnn_W_out), axis=-1)
    x = _layernorm(x + _L1_gnn_ref(x, adj, L1_gnn_W, L1_gnn_a), axis=-1)
    x = _layernorm(x + _L2_gnn_ref(x, adj, L2_gnn_Wq, L2_gnn_bq, L2_gnn_Wk, L2_gnn_bk, L2_gnn_Wv, L2_gnn_bv, L2_gnn_Wo, L2_gnn_bo, L2_gnn_gamma, L2_gnn_beta), axis=-1)
    x = _layernorm(x + _L3_gnn_ref(x, adj, L3_gnn_wq, L3_gnn_bq, L3_gnn_wk, L3_gnn_bk, L3_gnn_wv, L3_gnn_bv, L3_gnn_wo, L3_gnn_bo), axis=-1)
    return x

_drawn_inputs = setup_inputs


def setup_inputs(seed=0):
    import zlib

    import numpy as np

    out = dict(_drawn_inputs(seed))
    spreads = {'L2_gnn_bq': (0.0, 0.722),
     'L2_gnn_bk': (0.0, 2.0),
     'L2_gnn_bv': (0.0, 0.1),
     'L2_gnn_bo': (0.0, 0.381),
     'L2_gnn_gamma': (1.0, 0.2),
     'L2_gnn_beta': (0.0, 0.1)}
    factors = {'L3_gnn_bq': 8.0, 'L3_gnn_bk': 64.0}
    for name, (base, spread) in spreads.items():
        noise = np.random.default_rng([zlib.crc32(name.encode()), seed]).standard_normal(out[name].shape)
        drawn = base * np.exp(spread * noise) if base else spread * noise
        out[name] = jnp.asarray(drawn.astype(out[name].dtype))
    for name, factor in factors.items():
        out[name] = (out[name] * factor).astype(out[name].dtype)
    return out
```

```python
import math
from contextlib import ExitStack

import concourse.bass as bass
from concourse import mybir

F32 = mybir.dt.float32
F16 = mybir.dt.float16
BF16 = mybir.dt.bfloat16
I32 = mybir.dt.int32
ALU = mybir.AluOpType
ACT = mybir.ActivationFunctionType
AX = mybir.AxisListType

P = 128
LANES = 2
LAYERS = 4
PHASES = LANES * LAYERS
HALF = 512
EPS_LN = 1e-5
EPS_LOG = 1e-6
ABSENT = -1e30
HEADS = (8, 1, 4, 4)
SLOPE = (0.2, 0.01)
TAU_START = 80.0
CLIP = 10.0
HD = 32
SPLIT_ROWS = 3 * HD
RING = 8
LAG = (4, 0, 2, 2)
RHOS = 4


def phase_plan(NT):
    groups = {0: [4] * (2 * NT), 1: [1] * NT, 2: [2] * (2 * NT), 3: [2] * (2 * NT)}
    tile0, group0, group_of = [], [], []
    n_groups = 0
    for k in range(PHASES):
        tile0.append(len(group_of))
        group0.append(n_groups)
        for size in groups[k // LANES]:
            group_of += [n_groups] * size
            n_groups += 1
    return tile0, group0, group_of


def side_uses(k):
    uses = []
    if k >= 1:
        layer = (k - 1) // LANES
        uses += {0: ["den", "norm0", "norm1", "out"], 1: ["den", "out"],
                 2: ["out"], 3: ["den", "norm0", "out"]}[layer]
    if k + 1 < PHASES and k >= -1:
        layer = (k + 1) // LANES
        uses += ["xT"]
        uses += ["tops", "top_bc", "values0", "values1"] if layer < 2 else ["q", "k", "v"]
        if layer == 3:
            uses += [f"max{n}" for n in range(64)] + ["max_rows"]
    return uses


def stage_weight(name):
    if name.startswith("max"):
        return 1
    return {"out": 10, "k": 6, "v": 8}.get(name, 4)


def build(nc, x, adj, w0, a0s, a0d, beta0, wo0, w1, a1, w2, b2, gamma2, beta2, w3, b3, out):
    B, N, D = x.shape
    NT = N // P
    assert D == P and N == 2 * HALF and B % LANES == 0
    PAIRS = B // LANES
    tile0, group0, group_of = phase_plan(NT)
    QSCALE = float(HD) ** -0.5

    x_index = {}
    for k in range(-1, PHASES + 1):
        for name in side_uses(k):
            x_index[k, name] = len(x_index)

    def before(k, per_layer):
        return sum(per_layer[j // LANES] for j in range(k))

    def filled0(k):
        return before(k, (8 * NT, 0, 4 * NT, 4 * NT))

    def finished0(k):
        return before(k, (8 * NT, NT, 4 * NT, 0))

    def evac0(k):
        return before(k, (2, 2, 2 * NT, 2))

    def rho0(k):
        return before(k, (8, 1, 0, 0))

    def chunks0(k):
        return before(k, (0, 0, 2 * NT, 0))

    def added0(k):
        return before(k, (0, 0, 2 * NT - 2, 0))

    ctx = ExitStack()
    with ctx:
        def sb(name, shape, dt=F32):
            return ctx.enter_context(nc.sbuf_tensor(name, shape, dt))

        def ps(name, shape):
            return ctx.enter_context(nc.psum_tensor(name, shape, F32))

        all_sems = []

        def sem(name, looped=True):
            s = ctx.enter_context(nc.semaphore(name))
            if looped:
                all_sems.append(s)
            return s

        edge = sb("edge", [P, NT, N])
        absent = sb("absent", [P, NT, N], BF16)
        ring = sb("ring", [P, RING, N])
        rho = sb("rho", [P, RHOS, N])
        xn = [sb(f"xn{s}", [P, NT, P]) for s in range(LANES)]
        xT = [sb(f"xT{s}", [P, N]) for s in range(LANES)]
        U = [sb(f"U{s}", [P, 2, N]) for s in range(LANES)]
        qs = [sb(f"qs{s}", [P, 4, N], F16) for s in range(LANES)]
        ks = [sb(f"ks{s}", [P, 4, N], F16) for s in range(LANES)]
        vals = [sb(f"vals{s}", [P, NT, P]) for s in range(LANES)]
        tmp = sb("tmp", [P, NT, P])
        rexp = sb("rexp", [P, NT, P])
        hilo = sb("hilo", [P, 2, 2, N], F16)
        identf = sb("identf", [P, P])
        identb = sb("identb", [P, P], BF16)
        ones = sb("ones", [P, P])
        selD = sb("selD", [P, 1])
        mhalf = sb("mhalf", [P, NT])
        wcat = [sb(f"wcat{l}", [P, P + HEADS[l]]) for l in range(2)]
        wsd = [sb(f"wsd{l}", [P, 2 * HEADS[l]]) for l in range(2)]
        woutp = sb("woutp", [P, 2, P])
        wt = {(l, n): sb(f"w{n}T{l}", [P, P]) for l in (2, 3) for n in "qkvo"}
        bcol = {(l, n): sb(f"b{n}{l}", [P, 1]) for l in (2, 3) for n in "qk"}
        bvB = {l: sb(f"bv{l}", [P, P]) for l in (2, 3)}
        bo = {l: sb(f"bo{l}", [1, P]) for l in (2, 3)}
        gammaB = sb("gammaB", [P, P])
        betaB = sb("betaB", [P, P])
        mx = sb("mx", [16, 1])
        diag = sb("diag", [16, 16])
        tops = sb("tops", [P, 16])
        tau = sb("tau", [P, 8])
        rbias = [sb(f"rbias{s}", [P, 8]) for s in range(LANES)]
        kap = [sb(f"kap{s}", [P, 8]) for s in range(LANES)]
        nkap = [sb(f"nkap{s}", [P, 8]) for s in range(LANES)]
        wj = [sb(f"wj{s}", [P, NT, 8]) for s in range(LANES)]
        dm = sb("dm", [P, 4, 8])
        gj = sb("gj", [P, 4, 8])
        gcol = [sb(f"gcol{s}", [P, NT, 32]) for s in range(LANES)]
        rn = sb("rn", [P, 64])
        stats = sb("stats", [P, NT, 6])
        mv = sb("mv", [P, NT, 2])
        veps = sb("veps", [P, NT])
        rstd = sb("rstd", [P, NT])
        mpart = sb("mpart", [P, 32, 2])
        mcol = sb("mcol", [P, 32])
        mrow = sb("mrow", [32, P], F16)
        betac = sb("betac", [P, 4])
        psS = ps("psS", [P, 2, N])
        psU = ps("psU", [P, 2, HALF])
        psX = ps("psX", [P, N])

        vpad = [qs[s][:, :, :].bitcast(F32).rearrange("p a (b h f) -> p (a b) h f", h=8, f=32)
                for s in range(LANES)]

        chunk = rho[:, 1, :].rearrange("p (b n) -> p b n", b=2)
        rden = rho[:, 2, :].rearrange("p (b n) -> p b n", b=2)
        den_log = rho[:, 3, :].rearrange("p (b n) -> p b n", b=2)

        s_x_in = [sem(f"x_in{s}") for s in range(LANES)]
        s_zeroed = sem("vpad_zeroed")
        s_xw = sem("psX_written")
        s_xr = sem("psX_read")
        s_diag = sem("diag_ready")
        s_tau = sem("tau_ready")
        s_kap = sem("kappa_ready")
        s_nkap = sem("minus_kappa_ready")
        s_dm = sem("dst_minus_top_ready")
        s_wj = sem("w_and_g_ready")
        s_vals = sem("values_ready")
        s_rexp = sem("reciprocals_spread")
        s_norm = sem("sums_normalised")
        s_veps = sem("variance_ready")
        s_rstd = sem("rstd_ready")
        s_xn = sem("xn_ready")
        s_xT = sem("xT_ready")
        s_hi = sem("qk_full_and_hi_ready")
        s_lo = sem("qk_lo_ready")
        s_stack = {(l, s): sem(f"stacked{l}{s}") for l in (2, 3) for s in range(LANES)}
        s_mcol = sem("max_columns_ready")
        s_mrow = sem("max_rows_ready")
        s_rho_ps = sem("rho_in_psum")
        s_rho = sem("rho_ready")
        s_scores = sem("scores_ready")
        s_filled = sem("tile_filled")
        s_finished = sem("tile_finished")
        s_used = sem("tile_group_used")
        s_evac = sem("sums_out_of_psum")
        s_chain = sem("vector_chain")
        s_achain = sem("scalar_chain")
        s_den = sem("denominators_ready")
        s_rden = sem("chunk_reciprocals_ready")
        s_scaled = sem("chunk_normalised")
        s_added = sem("chunk_added")
        s_out = sem("stored")
        s_done = {e: sem(f"{e}_at_end") for e in ("pe", "act", "dve", "pool")}
        s_go = sem("pair_done", looped=False)
        s_load = sem("weights_loaded", looped=False)
        s_adj = sem("adj_loaded", looped=False)
        s_adjf = sem("adj_as_float", looped=False)
        s_adjT = sem("adj_transposed", looped=False)
        s_adjr = sem("adj_T_out", looped=False)
        s_ln = sem("log_ready", looped=False)
        s_pw = sem("power_ready", looped=False)
        s_edge = sem("edge_ready", looped=False)
        s_id = sem("identity_ready", looped=False)
        s_ones = sem("ones_ready", looped=False)
        s_wT = sem("weight_transposed", looped=False)
        s_wTr = sem("weight_T_out", looped=False)
        s_wpad = sem("wout_padded", looped=False)
        s_b = sem("beta_ready", looped=False)
        s_vset = sem("vector_setup_chain", looped=False)
        s_aset = sem("scalar_setup_chain", looped=False)
        s_setup = sem("setup_done", looped=False)

        adj_i = ring[:, 0:NT, :].bitcast(I32)
        adj_f = ring[:, 0:NT, :]
        stage = [t[:, :, :].bitcast(F32).rearrange("p a n -> p (a n)") for t in (*qs, *ks)]
        adj_eps = [stage[t // 2][:, (t % 2) * N:(t % 2 + 1) * N] for t in range(NT)]
        raw = {("o", 0): rho[:, 0, 0:P]}
        for i, key in enumerate([(n, l) for l in (2, 3) for n in "qkvo"]):
            raw[key] = rho[:, 1, i * P:(i + 1) * P]
        wpad = rho[:, 0, 256:512].rearrange("p (g q r) -> p g q r", g=2, q=4)
        a_row = {0: rho[:, 2, 0:256], 1: rho[:, 2, 256:512]}
        prod = rho[:, 3, 0:P]
        WEIGHTS = [("q", 2), ("k", 2), ("v", 2), ("o", 2), ("q", 3), ("k", 3), ("v", 3), ("o", 3)]

        def lane_of(k):
            return k % LANES

        def due(t, tiles, k):
            weights = [stage_weight(name) for name in side_uses(k)]
            return sum(sum(weights[:i]) * tiles < t * sum(weights) for i in range(len(weights)))

        def due_reader(t, tiles, k):
            group, lag = ((4, LAG[0]), (1, LAG[1]), (2, LAG[2]), (2, LAG[3]))[k // LANES]
            return due(max(0, t // group * group - lag), tiles, k)

        def chunks_before_norm(k):
            uses, tiles = side_uses(k), 4 * NT
            n = next(n for n in range(tiles) if due_reader(n + 1, tiles, k) > uses.index("out"))
            return (n - 1) // 2 if n >= 3 else 0

        block = ctx.enter_context(nc.Block())

        @block.sync
        def _(sp):
            loads = [
                (wcat[0][:, 0:P].rearrange("p (h f) -> p h f", h=8), w0.rearrange("h d f -> d h f")),
                (wcat[1][:, 0:P], w1),
                (a_row[0][:, 0:P], a0s.rearrange("(o h) f -> o (h f)", o=1).broadcast_to([P, P])),
                (a_row[0][:, P:2 * P], a0d.rearrange("(o h) f -> o (h f)", o=1).broadcast_to([P, P])),
                (a_row[1], a1.rearrange("n o -> o n").broadcast_to([P, 2 * P])),
                (raw["o", 0], wo0),
                (betac[:, 0:1], beta0.broadcast_to([P, 1])),
                (gammaB[:, :], gamma2.rearrange("(o n) -> o n", o=1).broadcast_to([P, P])),
                (betaB[:, :], beta2.rearrange("(o n) -> o n", o=1).broadcast_to([P, P])),
            ]
            for l, w, b in ((2, w2, b2), (3, w3, b3)):
                loads += [(raw[n, l], w[n]) for n in "qkvo"]
                loads += [(bcol[l, n][:, :], b[n].rearrange("(p o) -> p o", o=1)) for n in "qk"]
                loads += [(bvB[l][:, :], b["v"].rearrange("(o n) -> o n", o=1).broadcast_to([P, P])),
                          (bo[l][:, :], b["o"].rearrange("(o n) -> o n", o=1))]
            for dst, src in loads:
                sp.dma_start(dst, src).then_inc(s_load, 16)
            assert len(loads) == N_LOADS
            for t in range(NT):
                sp.dma_start(adj_i[:, t, :], adj[t * P:(t + 1) * P, :]).then_inc(s_adj, 16)

            with sp.Fori(0, PAIRS) as pair:
                for s in range(LANES):
                    sp.dma_start(xn[s][:, :, :], x[LANES * pair + s, :, :].rearrange("(t p) d -> p t d", p=P))\
                      .then_inc(s_x_in[s], 16)
                for k in range(2 * LANES, PHASES):
                    l, s = k // LANES, lane_of(k)
                    if l == 3:
                        sp.wait_ge(s_used, group0[k - LANES + 1])
                    for m, (dst, parts) in enumerate(((qs[s], (0, 0, 1)), (ks[s], (0, 1, 0)))):
                        sp.wait_ge(s_hi, 2 * (k - 4) + m + 1)
                        sp.wait_ge(s_lo, 2 * (k - 4) + m + 1)
                        for h in range(4):
                            for r, part in enumerate(parts):
                                sp.dma_start(dst[r * HD:(r + 1) * HD, h, :],
                                             hilo[h * HD:(h + 1) * HD, m, part, :]).then_inc(s_stack[l, s], 16)
                    if l == 3:
                        sp.wait_ge(s_mrow, k - 6 + 1)
                        sp.dma_start(qs[s][SPLIT_ROWS:SPLIT_ROWS + 1, :, :].rearrange("p h (t i) -> p (h t) i", i=P),
                                     mrow[:, :]).then_inc(s_stack[l, s], 16)
                for s in range(LANES):
                    sp.wait_ge(s_xn, 4 * LANES - 1 + s)
                    sp.dma_start(out[LANES * pair + s, :, :].rearrange("(t p) d -> p t d", p=P), xn[s][:, :, :])\
                      .then_inc(s_out, 16)
                sp.wait_ge(s_out, 16 * LANES)
                for e in s_done.values():
                    sp.wait_ge(e, 1)
                for q in all_sems:
                    sp.sem_clear(q)
                sp.sem_inc(s_go, 1)

        @block.gpsimd
        def _(pool):
            nc.gpsimd.memset(ones[:, :], 1.0).then_inc(s_ones, 1)
            nc.gpsimd.memset(mhalf[:, :], -0.5).then_inc(s_ones, 1)
            nc.gpsimd.memset(identf[:, :], 0.0).then_inc(s_id, 1)
            pool.wait_ge(s_id, 1)
            nc.gpsimd.affine_select(out=identf[:, :], in_=identf[:, :], compare_op=ALU.not_equal, fill=1.0,
                                    base=0, pattern=[[-1, P]], channel_multiplier=1).then_inc(s_id, 1)
            pool.wait_ge(s_id, 2)
            nc.gpsimd.tensor_copy(identb[:, :], identf[:, :]).then_inc(s_id, 1)
            pool.wait_ge(s_setup, 1)
            for s in range(LANES):
                nc.gpsimd.memset(ks[s][SPLIT_ROWS:SPLIT_ROWS + 1, :, :], 1.0).then_inc(s_id, 1)
                pool.wait_ge(s_id, 4 + s)

            with pool.Fori(0, PAIRS) as pair:
                for s in range(LANES):
                    nc.gpsimd.memset(vpad[s], 0.0).then_inc(s_zeroed, 1)
                    pool.wait_ge(s_zeroed, s + 1)
                norms = 0

                def rstds(count):
                    nonlocal norms
                    for _ in range(count):
                        norms += 1
                        pool.wait_ge(s_veps, norms)
                        nc.gpsimd.tensor_tensor(rstd[:, :], veps[:, :], mhalf[:, :], ALU.pow).then_inc(s_rstd, 1)

                for k in range(PHASES):
                    l, s = k // LANES, lane_of(k)
                    norms_in_side = 0 if k == 0 else 2 if (k - 1) // LANES == 2 else 1
                    if l == 2:
                        n_added = added0(k)
                        for n in range(2 * NT):
                            half = n // NT
                            if n == chunks_before_norm(k):
                                rstds(norms_in_side)
                            if n % NT:
                                pool.wait_ge(s_scaled, chunks0(k) + n + 1)
                                if n_added:
                                    pool.wait_ge(s_added, n_added)
                                part = U[s][:, 0, half * HALF:(half + 1) * HALF]
                                nc.gpsimd.tensor_tensor(part, part, chunk[:, n % 2, :], ALU.add).then_inc(s_added, 1)
                                n_added += 1
                    else:
                        rstds(norms_in_side)
                rstds(1)
                pool.sem_inc(s_done["pool"], 1)
                pool.wait_ge(s_go, pair + 1)

        @block.scalar
        def _(act):
            link_n = [0]

            def link(ins):
                link_n[0] += 1
                ins.then_inc(s_achain, 1)
                act.wait_ge(s_achain, link_n[0])

            act.wait_ge(s_load, 16 * N_LOADS)
            act.wait_ge(s_b, 1)
            act.wait_ge(s_ones, 2)
            nc.scalar.activation(betac[:, 2:3], betac[:, 1:2], ACT.Exp).then_inc(s_aset, 1)
            act.wait_ge(s_aset, 1)
            nc.scalar.activation(betac[:, 3:4], betac[:, 2:3], ACT.Ln, bias=ones[:, 0:1]).then_inc(s_aset, 1)
            for t in range(NT):
                act.wait_ge(s_adjr, t + 1)
                nc.scalar.activation(edge[:, t, :], adj_eps[t], ACT.Ln).then_inc(s_ln, 1)
            act.wait_ge(s_b, 2)
            act.wait_ge(s_ln, NT)
            for t in range(NT):
                nc.scalar.activation(edge[:, t, :], edge[:, t, :], ACT.Exp, scale=betac[:, 1:2]).then_inc(s_pw, 1)
            act.wait_ge(s_setup, 1)

            def gat_rho(k, h):
                l, s = k // LANES, lane_of(k)
                act.wait_ge(s_rho_ps, rho0(k) + h + 1)
                if h >= RHOS:
                    act.wait_ge(s_filled, filled0(k) + RHOS * NT)
                elif k >= 1:
                    act.wait_ge(s_filled, filled0(k))
                    act.wait_ge(s_finished, finished0(k))
                nc.scalar.activation(rho[:, h % RHOS, :], psS[:, (h + l) % 2, :], ACT.Exp,
                                     bias=rbias[s][:, h:h + 1], scale=1.0 - SLOPE[l]).then_inc(s_rho, 1)

            def side(k):
                for name in side_uses(k):
                    m = x_index[k, name]
                    s = lane_of(k + 1)
                    l = (k + 1) // LANES
                    n_gat = k + 1
                    if name == "xT":
                        act.wait_ge(s_xw, m + 1)
                        nc.scalar.activation(xT[s][:, :], psX[:, :], ACT.Copy).then_inc(s_xr, 1)
                    elif name == "top_bc":
                        act.wait_ge(s_tau, n_gat + 1)
                        nc.scalar.activation(kap[s][:, 0:HEADS[l]], tau[:, 0:HEADS[l]], ACT.Exp, scale=-1.0)\
                            .then_inc(s_kap, 1)
                    elif name in ("values0", "values1"):
                        half = int(name[-1])
                        H = HEADS[l]
                        act.wait_ge(s_dm, 2 * n_gat + half + 1)
                        nc.scalar.activation(wj[s][:, 4 * half:4 * half + 4, 0:H], dm[:, :, 0:H], ACT.Exp,
                                             scale=1.0 - SLOPE[l])
                        nc.scalar.activation(gj[:, :, 0:H], dm[:, :, 0:H], ACT.Exp, scale=SLOPE[l]).then_inc(s_wj, 1)
                    elif name in ("q", "k"):
                        q = name == "q"
                        act.wait_ge(s_xw, m + 1)
                        i = 2 * (k + 1 - 4) + (not q)
                        if i >= 1:
                            act.wait_ge(s_lo, i)
                        if i >= 2:
                            j = i // 2 - 1
                            act.wait_ge(s_stack[2 + j // LANES, j % LANES], 24 * 16)
                        nc.scalar.activation(tmp[:, :, :].rearrange("p a b -> p (a b)"), psX[:, :], ACT.Identity,
                                             bias=bcol[l, name][:, :], scale=QSCALE if q else 1.0).then_inc(s_xr, 1)
                        act.wait_ge(s_xr, m + 1)
                        nc.scalar.activation(hilo[:, 1 - q, 0, :], tmp[:, :, :].rearrange("p a b -> p (a b)"),
                                             ACT.Copy).then_inc(s_hi, 1)
                    elif name == "max_rows":
                        act.wait_ge(s_xw, m + 1)
                        nc.scalar.activation(mrow[:, :], psX[0:32, 0:P], ACT.Copy, scale=-1.0).then_inc(s_mrow, 1)
                        act.wait_ge(s_mrow, k + 1 - 6 + 1)
                        act.sem_inc(s_xr, 1)
                    yield

            def free_slot(t):
                if t >= RING:
                    act.wait_ge(s_used, group_of[t - RING] + 1)

            with act.Fori(0, PAIRS) as pair:
                link_n[0] = 0
                for _ in side(-1):
                    pass
                for k in range(PHASES):
                    l, s = k // LANES, lane_of(k)
                    stages = side(k)
                    done = 0
                    tiles = {0: 8 * NT, 1: NT, 2: 4 * NT, 3: 4 * NT}[l]

                    def advance(t):
                        nonlocal done
                        while done < due_reader(t, tiles, k):
                            next(stages)
                            done += 1

                    if l == 0:
                        act.wait_ge(s_nkap, k + 1)
                        n = 0
                        for g in range(2):
                            if g == 0:
                                for h in range(4):
                                    gat_rho(k, h)
                            for jt in range(NT):
                                for h in range(4 * g, 4 * g + 4):
                                    t = tile0[k] + n
                                    free_slot(t)
                                    act.wait_ge(s_rho, rho0(k) + h + 1)
                                    nc.scalar.activation(ring[:, t % RING, :], rho[:, h % RHOS, :], ACT.Relu,
                                                         bias=nkap[s][:, h:h + 1], scale=wj[s][:, jt, h:h + 1])\
                                        .then_inc(s_filled, 1)
                                    n += 1
                                    advance(n)
                            if g == 0:
                                for h in range(4, 8):
                                    gat_rho(k, h)
                            act.wait_ge(s_used, group0[k] + NT * (g + 1))
                            nc.scalar.activation(U[s][:, g, :], psU[:, :, :].rearrange("p a b -> p (a b)"),
                                                 ACT.Copy).then_inc(s_evac, 1)
                    elif l == 1:
                        act.wait_ge(s_nkap, k + 1)
                        gat_rho(k, 0)
                        for n in range(NT):
                            advance(n + 1)
                        act.wait_ge(s_used, group0[k] + NT)
                        nc.scalar.activation(U[s][:, 0, :], psU[:, :, :].rearrange("p a b -> p (a b)"),
                                             ACT.Copy).then_inc(s_evac, 1)
                        nc.scalar.activation(U[s][:, 1, :], psS[:, 0, :], ACT.Copy).then_inc(s_evac, 1)
                    else:
                        def reciprocals(n):
                            i = chunks0(k) + n
                            act.wait_ge(s_den, i + 1)
                            if i >= 2:
                                act.wait_ge(s_rden, i - 1)
                            nc.scalar.activation(den_log[:, n % 2, :], psU[:, 1, :], ACT.Ln).then_inc(s_evac, 1)
                            act.wait_ge(s_evac, evac0(k) + n + 1)
                            if i >= 2:
                                act.wait_ge(s_scaled, i - 1)
                            nc.scalar.activation(rden[:, n % 2, :], den_log[:, n % 2, :], ACT.Exp, scale=-1.0).then_inc(s_rden, 1)

                        def evacuate(half):
                            act.wait_ge(s_used, group0[k] + NT * (half + 1))
                            nc.scalar.activation(U[s][:, :, half * HALF:(half + 1) * HALF], psU[:, :, :],
                                                 ACT.Copy).then_inc(s_evac, 1)

                        for n in range(2 * NT):
                            for p in range(2):
                                t = tile0[k] + 2 * n + p
                                act.wait_ge(s_scores, 4 * NT * (k - 4) + 2 * n + p + 1)
                                free_slot(t)
                                nc.scalar.activation(ring[:, t % RING, :], psS[:, p, :], ACT.Exp).then_inc(s_filled, 1)
                                if l == 2 and n >= 1 and p == 1:
                                    reciprocals(n - 1)
                                if l == 3 and n == NT and p == 1:
                                    evacuate(0)
                                advance(2 * n + p + 1)
                        if l == 2:
                            reciprocals(2 * NT - 1)
                        else:
                            evacuate(1)
                    for _ in stages:
                        pass
                for _ in side(PHASES):
                    pass
                act.sem_inc(s_done["act"], 1)
                act.wait_ge(s_go, pair + 1)

        @block.vector
        def _(dve):
            link_n = [0]
            chain = [s_vset]

            def link(ins):
                link_n[0] += 1
                ins.then_inc(chain[0], 1)
                dve.wait_ge(chain[0], link_n[0])

            dve.wait_ge(s_load, 16 * N_LOADS)
            link(nc.vector.tensor_scalar(betac[:, 1:2], betac[:, 0:1], -1.0, None, ALU.mult))
            nc.vector.tensor_tensor(betac[:, 1:2], betac[:, 0:1], betac[:, 1:2], ALU.min).then_inc(s_b, 1)
            dve.wait_ge(s_aset, 2)
            nc.vector.scalar_tensor_tensor(betac[:, 1:2], betac[:, 0:1], 0.0, betac[:, 3:4], ALU.max, ALU.add)\
                .then_inc(s_b, 1)
            for l in range(2):
                H = HEADS[l]
                for side_ in range(2):
                    link(nc.vector.tensor_tensor(prod, wcat[l][:, 0:P], a_row[l][:, side_ * P:(side_ + 1) * P], ALU.mult))
                    link(nc.vector.tensor_reduce(wsd[l][:, side_ * H:(side_ + 1) * H],
                                                 prod.rearrange("p (h f) -> p h f", h=H), AX.X, ALU.add))
                link(nc.vector.tensor_copy(wcat[l][:, P:P + H], wsd[l][:, H:2 * H]))
            link(nc.vector.memset(rho[:, 0, 256:512], 0.0))
            nc.vector.tensor_copy(wpad[:, :, :, 0:16],
                                  raw["o", 0].rearrange("p (g q r) -> p g q r", g=2, q=4)).then_inc(s_wpad, 1)
            dve.wait_ge(s_id, 3)
            link(nc.vector.tensor_reduce(selD[:, :], identf[:, 0:P:32], AX.X, ALU.add))
            dve.wait_ge(s_adj, 16 * NT)
            for it in range(NT):
                nc.vector.tensor_copy(adj_f[:, it, :], adj_i[:, it, :]).then_inc(s_adjf, 1)
            for jt in range(NT):
                dve.wait_ge(s_adjT, jt + 1)
                nc.vector.tensor_scalar(absent[:, jt, :], psS[:, jt % 2, :], 0.0, ABSENT, ALU.is_equal, ALU.mult)
                nc.vector.tensor_scalar(adj_eps[jt], psS[:, jt % 2, :], 0.0, EPS_LOG, ALU.max, ALU.add)\
                    .then_inc(s_adjr, 1)
            for i, (n, l) in enumerate(WEIGHTS):
                dve.wait_ge(s_wT, i + 1)
                nc.vector.tensor_copy(wt[l, n][:, :], psX[:, (i % 2) * HALF:(i % 2) * HALF + P]).then_inc(s_wTr, 1)
            for g in range(2):
                i = len(WEIGHTS) + g
                dve.wait_ge(s_wT, i + 1)
                nc.vector.tensor_copy(woutp[:, g, :], psX[:, (i % 2) * HALF:(i % 2) * HALF + P]).then_inc(s_wTr, 1)
            for l in (2, 3):
                link(nc.vector.tensor_scalar(bcol[l, "q"][:, :], bcol[l, "q"][:, :], QSCALE, None, ALU.mult))
            for t in range(NT):
                dve.wait_ge(s_pw, t + 1)
                link(nc.vector.scalar_tensor_tensor(edge[:, t, :], adj_eps[t], EPS_LOG, edge[:, t, :],
                                                    ALU.is_gt, ALU.mult))
            nc.vector.memset(veps[:, :], 0.0).then_inc(s_setup, 1)
            chain[0] = s_chain

            def gat_prologue(k, name, m):
                l, s = (k + 1) // LANES, lane_of(k + 1)
                n, H, lam = k + 1, HEADS[l], 1.0 - SLOPE[l]
                if name == "tops":
                    dve.wait_ge(s_xw, m + 1)
                    nc.vector.tensor_reduce(mx[0:2 * H, :], psX[0:2 * H, :], AX.X, ALU.max).then_inc(s_xr, 1)
                    dve.wait_ge(s_xr, m + 1)
                    nc.vector.tensor_scalar(diag[0:2 * H, 0:2 * H], identf[0:2 * H, 0:2 * H], mx[0:2 * H, :], None,
                                            ALU.mult).then_inc(s_diag, 1)
                elif name == "top_bc":
                    dve.wait_ge(s_xw, m + 1)
                    nc.vector.tensor_copy(tops[:, 0:2 * H], psX[:, 0:2 * H]).then_inc(s_xr, 1)
                    dve.wait_ge(s_xr, m + 1)
                    link(nc.vector.tensor_tensor(tau[:, 0:H], tops[:, 0:H], tops[:, H:2 * H], ALU.add))
                    link(nc.vector.tensor_scalar(tau[:, 0:H], tau[:, 0:H], lam, -TAU_START, ALU.mult, ALU.add))
                    link(nc.vector.tensor_scalar(tau[:, 0:H], tau[:, 0:H], 0.0, None, ALU.max))
                    nc.vector.scalar_tensor_tensor(rbias[s][:, 0:H], tops[:, H:2 * H], lam, tau[:, 0:H],
                                                   ALU.mult, ALU.subtract).then_inc(s_tau, 1)
                    dve.wait_ge(s_kap, n + 1)
                    nc.vector.tensor_scalar(nkap[s][:, 0:H], kap[s][:, 0:H], -1.0, None, ALU.mult).then_inc(s_nkap, 1)
                else:
                    half = int(name[-1])
                    jts = slice(4 * half, 4 * half + 4)
                    dve.wait_ge(s_xw, m + 1)
                    if 2 * n + half >= 1:
                        dve.wait_ge(s_wj, 2 * n + half)
                    v = psX[:, :].rearrange("p (t c) -> p t c", c=2 * P)
                    nc.vector.tensor_tensor(dm[:, :, 0:H], v[:, :, P:P + H],
                                            tops[:, H:2 * H].unsqueeze(1).broadcast_to([P, 4, H]), ALU.subtract)\
                        .then_inc(s_dm, 1)
                    dve.wait_ge(s_wj, 2 * n + half + 1)
                    if l == 0:
                        if half == 0:
                            dve.wait_ge(s_zeroed, s + 1)
                        nc.vector.tensor_copy(vpad[s][:, jts, :, 16:17], gj[:, :, 0:H].unsqueeze(3)).then_inc(s_vals, 1)
                        nc.vector.tensor_tensor(vpad[s][:, jts, :, 0:16],
                                                v[:, :, 0:P].rearrange("p t (h f) -> p t h f", h=H),
                                                gj[:, :, 0:H].unsqueeze(3).broadcast_to([P, 4, H, 16]), ALU.mult)\
                            .then_inc(s_xr, 1)
                    else:
                        nc.vector.tensor_copy(gcol[s][:, jts, :], gj[:, :, 0:1].broadcast_to([P, 4, 32]))\
                            .then_inc(s_vals, 1)
                        nc.vector.tensor_tensor(vals[s][:, jts, :], v[:, :, 0:P],
                                                gj[:, :, 0:1].broadcast_to([P, 4, P]), ALU.mult).then_inc(s_xr, 1)

            norms = [0]

            def normalise(dst, src):
                for t in range(NT):
                    ins = nc.vector.bn_stats(stats[:, t, :], src[:, t, :])
                link(ins)
                for t in range(NT):
                    ins = nc.vector.bn_aggr(mv[:, t, :], stats[:, t, :])
                link(ins)
                norms[0] += 1
                nc.vector.tensor_scalar(veps[:, :], mv[:, :, 1], EPS_LN, None, ALU.add).then_inc(s_veps, 1)
                dve.wait_ge(s_rstd, norms[0])
                for t in range(NT):
                    ins = nc.vector.tensor_scalar(dst[:, t, :], src[:, t, :], mv[:, t, 0:1], rstd[:, t:t + 1],
                                                  ALU.subtract, ALU.mult)
                return ins

            def epilogue(k, name, m):
                l, s = (k - 1) // LANES, lane_of(k - 1)
                ps3 = psX[:, :].rearrange("p (t d) -> p t d", d=P)
                dve.wait_ge(s_xw, m + 1)

                def spread(col0, per):
                    nc.vector.tensor_copy(rexp[:, :, :].rearrange("p t (h r) -> p t h r", h=4),
                                          rn[:, 0:NT * per].rearrange("p (t h) -> p t h", h=per)[:, :, col0:col0 + 4]
                                          .unsqueeze(3).broadcast_to([P, NT, 4, 32])).then_inc(s_rexp, 1)

                if name == "den":
                    per = {0: 8, 1: 1, 2: 4, 3: 4}[l]
                    if l == 3:
                        nc.vector.tensor_scalar(rn[:, 0:NT * per], psX[:, 0:NT * per], 1e-37, None, ALU.max)\
                            .then_inc(s_xr, 1)
                        dve.wait_ge(s_xr, m + 1)
                        link(nc.vector.reciprocal(rn[:, 0:NT * per], rn[:, 0:NT * per]))
                    else:
                        nc.vector.reciprocal(rn[:, 0:NT * per], psX[:, 0:NT * per]).then_inc(s_xr, 1)
                        dve.wait_ge(s_xr, m + 1)
                    if l != 1:
                        spread(0, per)
                elif name in ("norm0", "norm1"):
                    g = int(name[-1])
                    nc.vector.tensor_tensor(U[s][:, g, :], U[s][:, g, :], psX[:, :], ALU.mult).then_inc(s_xr, 1)
                    if l == 0 and g == 0:
                        spread(4, 8)
                elif name == "out":
                    if l == 1:
                        nc.vector.scalar_tensor_tensor(tmp[:, :, :], ps3, 0.0,
                                                       rn[:, 0:NT].unsqueeze(2).broadcast_to([P, NT, P]),
                                                       ALU.max, ALU.mult).then_inc(s_xr, 1)
                        dve.wait_ge(s_xr, m + 1)
                        link(nc.vector.tensor_tensor(tmp[:, :, :], tmp[:, :, :], xn[s][:, :, :], ALU.add))
                    else:
                        nc.vector.tensor_tensor(tmp[:, :, :], ps3, xn[s][:, :, :], ALU.add).then_inc(s_xr, 1)
                        dve.wait_ge(s_xr, m + 1)
                    if l == 2:
                        link(normalise(tmp, tmp))
                        link(nc.vector.tensor_tensor(tmp[:, :, :], tmp[:, :, :],
                                                     gammaB[:, :].unsqueeze(1).broadcast_to([P, NT, P]), ALU.mult))
                        link(nc.vector.tensor_tensor(tmp[:, :, :], tmp[:, :, :],
                                                     betaB[:, :].unsqueeze(1).broadcast_to([P, NT, P]), ALU.add))
                        link(nc.vector.tensor_tensor(tmp[:, :, :], tmp[:, :, :], xn[s][:, :, :], ALU.add))
                    normalise(xn[s], tmp).then_inc(s_xn, 1)

            def side(k):
                n_epilogue = len(side_uses(k)) - (len(side_uses(-1)) if k == -1 else 0)
                names = side_uses(k)
                in_epilogue = k >= 1
                for name in names:
                    m = x_index[k, name]
                    if name == "xT":
                        in_epilogue = False
                    l, s = (k + 1) // LANES, lane_of(k + 1)
                    if in_epilogue:
                        epilogue(k, name, m)
                    elif name in ("tops", "top_bc", "values0", "values1"):
                        gat_prologue(k, name, m)
                    elif name in ("q", "k"):
                        q = name == "q"
                        i = 2 * (k + 1 - 4) + (not q)
                        dve.wait_ge(s_hi, i + 1)
                        if i >= 2:
                            j = i // 2 - 1
                            dve.wait_ge(s_stack[2 + j // LANES, j % LANES], 24 * 16)
                        nc.vector.tensor_tensor(hilo[:, 1 - q, 1, :], tmp[:, :, :].rearrange("p a b -> p (a b)"),
                                                hilo[:, 1 - q, 0, :], ALU.subtract).then_inc(s_lo, 1)
                    elif name == "v":
                        dve.wait_ge(s_xw, m + 1)
                        nc.vector.tensor_tensor(vals[s][:, :, :], psX[:, :].rearrange("p (t d) -> p t d", d=P),
                                                bvB[l][:, :].unsqueeze(1).broadcast_to([P, NT, P]), ALU.add)\
                            .then_inc(s_xr, 1)
                    elif name.startswith("max") and name != "max_rows":
                        i = int(name[3:])
                        dve.wait_ge(s_xw, m + 1)
                        nc.vector.tensor_reduce(mpart[:, i // 2, i % 2:i % 2 + 1],
                                                psX[:, (i % 2) * HALF:(i % 2 + 1) * HALF], AX.X, ALU.max)\
                            .then_inc(s_xr, 1)
                        if i == 63:
                            dve.wait_ge(s_xr, m + 1)
                            nc.vector.tensor_reduce(mcol[:, :], mpart[:, :, :], AX.X, ALU.max).then_inc(s_mcol, 1)
                    yield

            def normalise_chunk(k, n):
                s, half, i = lane_of(k), n // NT, chunks0(k) + n
                dve.wait_ge(s_used, group0[k] + n + 1)
                dve.wait_ge(s_rden, i + 1)
                if n >= 2:
                    dve.wait_ge(s_added, added0(k) + sum(1 for j in range(n - 1) if j % NT))
                elif k == 5:
                    dve.wait_ge(s_added, added0(k))
                dst = chunk[:, n % 2, :] if n % NT else U[s][:, 0, half * HALF:(half + 1) * HALF]
                nc.vector.tensor_tensor(dst, psU[:, 0, :], rden[:, n % 2, :], ALU.mult).then_inc(s_scaled, 1)

            with dve.Fori(0, PAIRS) as pair:
                link_n[0] = 0
                norms[0] = 0
                for _ in side(-1):
                    pass
                for k in range(PHASES):
                    l, s = k // LANES, lane_of(k)
                    stages = side(k)
                    done = 0
                    tiles = {0: 8 * NT, 1: NT, 2: 4 * NT, 3: 4 * NT}[l]
                    for n in range(tiles):
                        t = tile0[k] + n
                        slot = ring[:, t % RING, :]
                        if l == 0:
                            g, jt, h = n // 32, n % 32 // 4, n // 32 * 4 + n % 4
                            dve.wait_ge(s_filled, filled0(k) + n + 1)
                            nc.vector.scalar_tensor_tensor(slot, slot, kap[s][:, h:h + 1], edge[:, jt, :],
                                                           ALU.add, ALU.mult).then_inc(s_finished, 1)
                        elif l == 1:
                            if n == 0:
                                dve.wait_ge(s_rho, rho0(k) + 1)
                            dve.wait_ge(s_used, group_of[t - RING] + 1)
                            link(nc.vector.tensor_scalar(slot, rho[:, 0, :], wj[s][:, n, 0:1], kap[s][:, 0:1],
                                                         ALU.mult, ALU.max))
                            nc.vector.scalar_tensor_tensor(slot, absent[:, n, :], 0.0, slot,
                                                           ALU.is_equal, ALU.mult).then_inc(s_finished, 1)
                        elif l == 2:
                            dve.wait_ge(s_filled, filled0(k) + n + 1)
                            nc.vector.tensor_scalar(slot, slot, math.exp(-CLIP), math.exp(CLIP), ALU.max, ALU.min)\
                                .then_inc(s_finished, 1)
                            if n % 2 and n >= 3:
                                normalise_chunk(k, n // 2 - 1)
                        while done < due_reader(n + 1, tiles, k):
                            next(stages)
                            done += 1
                    if l == 2:
                        normalise_chunk(k, 2 * NT - 1)
                    for _ in stages:
                        pass
                for _ in side(PHASES):
                    pass
                dve.sem_inc(s_done["dve"], 1)
                dve.wait_ge(s_go, pair + 1)

        @block.tensor
        def _(pe):
            mm = nc.tensor.matmul

            pe.wait_ge(s_id, 3)
            pe.wait_ge(s_adjf, NT)
            for jt in range(NT):
                if jt >= 2:
                    pe.wait_ge(s_adjr, jt - 1)
                for it in range(NT):
                    ins = nc.tensor.transpose(psS[:, jt % 2, it * P:(it + 1) * P],
                                              adj_f[:, it, jt * P:(jt + 1) * P], identf[:, :])
                ins.then_inc(s_adjT, 1)
            pe.wait_ge(s_load, 16 * N_LOADS)
            for i, (n, l) in enumerate(WEIGHTS):
                if i >= 2:
                    pe.wait_ge(s_wTr, i - 1)
                nc.tensor.transpose(psX[:, (i % 2) * HALF:(i % 2) * HALF + P], raw[n, l], identf[:, :]).then_inc(s_wT, 1)
            pe.wait_ge(s_wpad, 1)
            for g in range(2):
                i = len(WEIGHTS) + g
                pe.wait_ge(s_wTr, i - 1)
                nc.tensor.transpose(psX[:, (i % 2) * HALF:(i % 2) * HALF + P],
                                    wpad[:, g, :, :].rearrange("p q r -> p (q r)"), identf[:, :]).then_inc(s_wT, 1)
            pe.wait_ge(s_wTr, len(WEIGHTS) + 2)
            pe.wait_ge(s_setup, 1)
            pe.wait_ge(s_id, 5)

            def side(k):
                in_epilogue = k >= 1
                for name in side_uses(k):
                    m = x_index[k, name]
                    if name == "xT":
                        in_epilogue = False
                    j = k - 1 if in_epilogue else k + 1
                    l, s = j // LANES, lane_of(j)
                    turns = name.startswith("max") and name not in ("max0", "max_rows")
                    if m - turns >= 1:
                        pe.wait_ge(s_xr, m - turns)

                    if name == "den":
                        pe.wait_ge(s_evac, evac0(j) + 2)
                        if l == 0:
                            for t in range(NT):
                                for g in range(2):
                                    ins = mm(psX[:, t * 8 + g * 4:t * 8 + g * 4 + 4], U[s][:, g, t * P:(t + 1) * P],
                                             identf[:, 16:P:32], start=True, stop=True)
                        elif l == 1:
                            for t in range(NT):
                                ins = mm(psX[:, t:t + 1], U[s][:, 1, t * P:(t + 1) * P], selD[:, :],
                                         start=True, stop=True)
                        else:
                            for t in range(NT):
                                ins = mm(psX[:, t * 4:t * 4 + 4], U[s][:, 1, t * P:(t + 1) * P],
                                         identf[:, 0:P:32], start=True, stop=True)
                    elif name in ("norm0", "norm1"):
                        n_before = before(j, (2, 0, 0, 1))
                        pe.wait_ge(s_rexp, n_before + int(name[-1]) + 1)
                        for t in range(NT):
                            ins = mm(psX[:, t * P:(t + 1) * P], rexp[:, t, :], identf[:, :], start=True, stop=True)
                    elif name == "out":
                        if l == 2:
                            pe.wait_ge(s_added, added0(j + 1))
                        for t in range(NT):
                            o = psX[:, t * P:(t + 1) * P]
                            if l == 0:
                                mm(o, U[s][:, 0, t * P:(t + 1) * P], woutp[:, 0, :], start=True, stop=False)
                                ins = mm(o, U[s][:, 1, t * P:(t + 1) * P], woutp[:, 1, :], start=False, stop=True)
                            elif l == 1:
                                ins = nc.tensor.transpose(o, U[s][:, 0, t * P:(t + 1) * P], identf[:, :])
                            else:
                                mm(o, U[s][:, 0, t * P:(t + 1) * P], wt[l, "o"][:, :], start=True, stop=False)
                                ins = mm(o, ones[0:1, :], bo[l][:, :], start=False, stop=True)
                    elif name == "xT":
                        if l == 0:
                            pe.wait_ge(s_x_in[s], 16)
                        else:
                            pe.wait_ge(s_xn, k)
                        for t in range(NT):
                            ins = nc.tensor.transpose(psX[:, t * P:(t + 1) * P], xn[s][:, t, :], identf[:, :])
                    elif name == "tops":
                        H = HEADS[l]
                        for i in range(2):
                            ins = mm(psX[0:2 * H, i * HALF:(i + 1) * HALF], wsd[l][:, :],
                                     xT[s][:, i * HALF:(i + 1) * HALF], start=True, stop=True)
                    elif name == "top_bc":
                        H = HEADS[l]
                        pe.wait_ge(s_diag, k + 2)
                        ins = mm(psX[:, 0:2 * H], ones[0:2 * H, :], diag[0:2 * H, 0:2 * H], start=True, stop=True)
                    elif name in ("values0", "values1"):
                        for i in range(4):
                            t = 4 * int(name[-1]) + i
                            ins = mm(psX[:, i * 2 * P:i * 2 * P + P + HEADS[l]], xT[s][:, t * P:(t + 1) * P],
                                     wcat[l][:, :], start=True, stop=True)
                    elif name in ("q", "k"):
                        for i in range(2):
                            ins = mm(psX[:, i * HALF:(i + 1) * HALF], wt[l, name][:, :],
                                     xT[s][:, i * HALF:(i + 1) * HALF], start=True, stop=True)
                    elif name == "v":
                        for t in range(NT):
                            ins = mm(psX[:, t * P:(t + 1) * P], xT[s][:, t * P:(t + 1) * P], wt[l, "v"][:, :],
                                     start=True, stop=True)
                    elif name == "max_rows":
                        pe.wait_ge(s_mcol, j - 6 + 1)
                        ins = nc.tensor.transpose(psX[0:32, 0:P], mcol[:, :], identf[:, :])
                    else:
                        i = int(name[3:])
                        if i == 0:
                            pe.wait_ge(s_stack[l, s], 24 * 16)
                        h, t, jh = i // 16, i % 16 // 2, i % 2
                        ins = mm(psX[:, jh * HALF:(jh + 1) * HALF], qs[s][0:SPLIT_ROWS, h, t * P:(t + 1) * P],
                                 ks[s][0:SPLIT_ROWS, h, jh * HALF:(jh + 1) * HALF], start=True, stop=True)
                    ins.then_inc(s_xw, 1)
                    yield

            with pe.Fori(0, PAIRS) as pair:
                for _ in side(-1):
                    pass
                for k in range(PHASES):
                    l, s = k // LANES, lane_of(k)
                    stages = side(k)
                    done = 0
                    tiles = {0: 8 * NT, 1: NT, 2: 4 * NT, 3: 4 * NT}[l]

                    def advance(t):
                        nonlocal done
                        while done < due(t, tiles, k):
                            next(stages)
                            done += 1

                    if k >= 1:
                        pe.wait_ge(s_evac, evac0(k))
                        pe.wait_ge(s_filled, filled0(k))
                        pe.wait_ge(s_rho, rho0(k))
                        if chunks0(k):
                            pe.wait_ge(s_scaled, chunks0(k))
                    if l < 2:
                        pe.wait_ge(s_xr, x_index[k - 1, "values1"] + 1)

                        def rho_rows(h):
                            if h >= 2:
                                pe.wait_ge(s_rho, rho0(k) + h - 1)
                            for i in range(2):
                                ins = mm(psS[:, (h + l) % 2, i * HALF:(i + 1) * HALF], wsd[l][:, h:h + 1].broadcast_to([P, P]),
                                         xT[s][:, i * HALF:(i + 1) * HALF], start=True, stop=True)
                            ins.then_inc(s_rho_ps, 1)

                    if l == 0:
                        for h in range(6):
                            rho_rows(h)
                        for g in range(2):
                            if g == 1:
                                rho_rows(6)
                                rho_rows(7)
                                pe.wait_ge(s_evac, evac0(k) + 1)
                            for jt in range(NT):
                                n = 4 * (g * NT + jt)
                                pe.wait_ge(s_finished, finished0(k) + n + 4)
                                for i in range(2):
                                    for q in range(4):
                                        t = tile0[k] + n + q
                                        ins = mm(psU[q * 32:(q + 1) * 32, i, :], vpad[s][:, jt, 4 * g + q, :],
                                                 ring[:, t % RING, i * HALF:(i + 1) * HALF],
                                                 start=(jt == 0), stop=(jt == NT - 1))
                                ins.then_inc(s_used, 1)
                                advance(n + 4)
                    elif l == 1:
                        rho_rows(0)
                        for jt in range(NT):
                            t = tile0[k] + jt
                            q = jt % 4
                            pe.wait_ge(s_finished, finished0(k) + jt + 1)
                            for i in range(2):
                                tile = ring[:, t % RING, i * HALF:(i + 1) * HALF]
                                mm(psU[:, i, :], vals[s][:, jt, :], tile, start=(jt == 0), stop=(jt == NT - 1))
                                ins = mm(psS[q * 32:(q + 1) * 32, 0, i * HALF:(i + 1) * HALF], gcol[s][:, jt, :], tile,
                                         start=(jt < 4), stop=(jt >= 4))
                            ins.then_inc(s_used, 1)
                            advance(jt + 1)
                    else:
                        rows = SPLIT_ROWS + (l == 3)
                        pe.wait_ge(s_stack[l, s], (24 + (l == 3)) * 16)
                        pe.wait_ge(s_xr, x_index[k - 1, "v"] + 1)

                        def scores(n):
                            half, jt = n // NT, n % NT
                            cols = slice(half * HALF, (half + 1) * HALF)
                            for p in range(2):
                                if n >= 1:
                                    pe.wait_ge(s_filled, filled0(k) + 2 * (n - 1) + p + 1)
                                for i in range(2):
                                    o = psS[:, p, i * HALF:(i + 1) * HALF]
                                    h = 2 * p + i
                                    mm(o, ks[s][0:rows, h, jt * P:(jt + 1) * P], qs[s][0:rows, h, cols],
                                       start=True, stop=False)
                                    ins = mm(o, identb[:, :], absent[:, jt, cols], start=False, stop=True)
                                ins.then_inc(s_scores, 1)

                        def sums(n):
                            half, jt = n // NT, n % NT
                            if l == 2 and n >= 1:
                                pe.wait_ge(s_evac, evac0(k) + n)
                            if l == 3 and n == NT:
                                pe.wait_ge(s_evac, evac0(k) + 1)
                            if l == 2:
                                pe.wait_ge(s_finished, finished0(k) + 2 * n + 2)
                            else:
                                pe.wait_ge(s_filled, filled0(k) + 2 * n + 2)
                            for bank in (1, 0):
                                if l == 2 and n >= 1 and bank == 0:
                                    pe.wait_ge(s_scaled, chunks0(k) + n)
                                for h in range(4):
                                    t = tile0[k] + 2 * n + h // 2
                                    w = ones[:, 0:HD] if bank else vals[s][:, jt, h * HD:(h + 1) * HD]
                                    ins = mm(psU[h * 32:(h + 1) * 32, bank, :], w,
                                             ring[:, t % RING, (h % 2) * HALF:(h % 2 + 1) * HALF],
                                             start=(l == 2 or jt == 0), stop=(l == 2 or jt == NT - 1))
                                if l == 2 and bank == 1:
                                    ins.then_inc(s_den, 1)
                            ins.then_inc(s_used, 1)

                        scores(0)
                        for n in range(2 * NT):
                            if n + 1 < 2 * NT:
                                scores(n + 1)
                            sums(n)
                            advance(2 * n + 2)
                for _ in side(PHASES):
                    pass
                pe.sem_inc(s_done["pe"], 1)
                pe.wait_ge(s_go, pair + 1)


N_LOADS = 9 + 2 * (4 + 2 + 2)

_INS = ['x', 'adj', 'L0_gnn_W', 'L0_gnn_a_src', 'L0_gnn_a_dst', 'L0_gnn_beta_tilde', 'L0_gnn_W_out', 'L1_gnn_W',
        'L1_gnn_a', 'L2_gnn_Wq', 'L2_gnn_bq', 'L2_gnn_Wk', 'L2_gnn_bk', 'L2_gnn_Wv', 'L2_gnn_bv', 'L2_gnn_Wo',
        'L2_gnn_bo', 'L2_gnn_gamma', 'L2_gnn_beta', 'L3_gnn_wq', 'L3_gnn_bq', 'L3_gnn_wk', 'L3_gnn_bk', 'L3_gnn_wv',
        'L3_gnn_bv', 'L3_gnn_wo', 'L3_gnn_bo']


def program(nc, t, out):
    build(nc, t["x"], t["adj"], t["L0_gnn_W"], t["L0_gnn_a_src"], t["L0_gnn_a_dst"], t["L0_gnn_beta_tilde"],
          t["L0_gnn_W_out"], t["L1_gnn_W"], t["L1_gnn_a"],
          {n: t[f"L2_gnn_W{n}"] for n in "qkvo"}, {n: t[f"L2_gnn_b{n}"] for n in "qkvo"},
          t["L2_gnn_gamma"], t["L2_gnn_beta"],
          {n: t[f"L3_gnn_w{n}"] for n in "qkvo"}, {n: t[f"L3_gnn_b{n}"] for n in "qkvo"}, out)


def kernel(**inputs):
    import numpy as _np
    import concourse.bacc as _bacc
    from concourse import mybir as _mybir
    from concourse.bass_utils import run_bass_kernel_spmd as _run

    nc = _bacc.Bacc("TRN2", target_bir_lowering=False, num_devices=1)
    arrays, args = {}, {}
    for name in _INS:
        a = _np.ascontiguousarray(inputs[name])
        if a.ndim == 0:
            a = a.reshape(1, 1)
        arrays[f"in_{name}_dram"] = a
        args[name] = nc.dram_tensor(f"in_{name}_dram", a.shape, _mybir.dt.from_np(a.dtype), kind="ExternalInput").ap()
    out = nc.dram_tensor("out_dram", inputs["x"].shape, _mybir.dt.float32, kind="ExternalOutput").ap()
    program(nc, args, out)
    r = _run(nc, [arrays], core_ids=[0])
    return r.results[0]["out_dram"]
```

```python
import math
from contextlib import ExitStack

import concourse.bass as bass
from concourse import mybir

F32 = mybir.dt.float32
F16 = mybir.dt.float16
BF16 = mybir.dt.bfloat16
I32 = mybir.dt.int32
ALU = mybir.AluOpType
ACT = mybir.ActivationFunctionType
AX = mybir.AxisListType

P = 128
LANES = 2
LAYERS = 4
PHASES = LANES * LAYERS
HALF = 512
EPS_LN = 1e-5
EPS_LOG = 1e-6
ABSENT = -1e30
HEADS = (8, 1, 4, 4)
SLOPE = (0.2, 0.01)
TAU_START = 80.0
CLIP = 10.0
HD = 32
SPLIT_ROWS = 3 * HD
RING = 8
LONG_RING = 12
LAG = {"act": (12, 12, 0, 0, 2, 0, 0, 0), "dve": (8, 8, 0, 0, 2, 0, 0, 0)}
RHOS = 6


def phase_plan(NT):
    groups = {0: [4] * (2 * NT), 1: [1] * NT, 2: [2] * (2 * NT), 3: [2] * (2 * NT)}
    tile0, group0, group_of = [], [], []
    n_groups = 0
    for k in range(PHASES):
        tile0.append(len(group_of))
        group0.append(n_groups)
        for size in groups[k // LANES]:
            group_of += [n_groups] * size
            n_groups += 1
    return tile0, group0, group_of


def ring_slots(tile0, n_tiles):
    slots, before, last = [], [], {}
    for t in range(n_tiles):
        slot = t % (LONG_RING if t < tile0[LANES] else RING)
        slots.append(slot)
        before.append(last.get(slot))
        last[slot] = t
    return slots, before


def side_uses(k):
    uses = []
    if k >= 1:
        layer = (k - 1) // LANES
        uses += {0: ["norm", "out"], 1: ["den", "out"], 2: ["out"], 3: ["norm", "out"]}[layer]
    if k + 1 < PHASES and k >= -1:
        layer = (k + 1) // LANES
        uses += ["xT"]
        uses += (["tops", "top_bc", "kappa", "values0", "g0", "values1", "g1"] if layer < 2 else ["q", "k", "v"])
        if layer == 3:
            uses += [f"max{n}" for n in range(64)] + ["max_rows"]
    return uses


def uses_psX(name):
    return name not in ("norm", "kappa", "g0", "g1")


WEIGHTS_OF = [dict(out=10), dict(out=10), dict(out=10), dict(out=10, k=6, v=8),
              dict(den=3, out=10, xT=2, k=10, v=8), dict(out=16, xT=5, k=6, v=16),
              dict(out=40, q=2, k=6, v=8, max_rows=3), dict(out=10)]
PAIR_FROM = 8
POINTS = (1, 1, 1, 1, 1, 4, 4, 4)


def stage_weight(k, name):
    if name.startswith("max"):
        return 1
    return WEIGHTS_OF[min(max(k, 0), PHASES - 1)].get(name, 4)


def build(nc, x, adj, w0, a0s, a0d, beta0, wo0, w1, a1, w2, b2, gamma2, beta2, w3, b3, out):
    B, N, D = x.shape
    NT = N // P
    assert D == P and N == 2 * HALF and B % LANES == 0
    PAIRS = B // LANES
    tile0, group0, group_of = phase_plan(NT)
    slot_of, tile_before = ring_slots(tile0, len(group_of))
    QSCALE = float(HD) ** -0.5

    x_index = {}
    for k in range(-1, PHASES + 1):
        for name in filter(uses_psX, side_uses(k)):
            x_index[k, name] = len(x_index)

    def before(k, per_layer):
        return sum(per_layer[j // LANES] for j in range(k))

    def filled0(k):
        return before(k, (8 * NT, 0, 4 * NT, 4 * NT))

    def finished0(k):
        return before(k, (8 * NT, NT, 4 * NT, 0))

    def evac0(k):
        return before(k, (2, 2, 2 * NT, 4))

    def rho0(k):
        return before(k, (8, 1, 0, 0))

    def accumulated0(k):
        return before(k, (0, 0, 0, 2 * (NT - 1)))

    def chunks0(k):
        return before(k, (0, 0, 2 * NT, 0))

    def added0(k):
        return before(k, (0, 0, 2 * NT - 2, 0))

    def rho_at(k, h):
        return {2: 4, 3: 0}[k] if k >= LANES else (h + 2 * k) % RHOS

    ctx = ExitStack()
    with ctx:
        def sb(name, shape, dt=F32):
            return ctx.enter_context(nc.sbuf_tensor(name, shape, dt))

        def ps(name, shape):
            return ctx.enter_context(nc.psum_tensor(name, shape, F32))

        all_sems = []

        def sem(name, looped=True):
            s = ctx.enter_context(nc.semaphore(name))
            if looped:
                all_sems.append(s)
            return s

        edge = sb("edge", [P, NT, N])
        absent = sb("absent", [P, NT, N], BF16)
        ring = sb("ring", [P, RING, N])
        rho = sb("rho", [P, 4, N])
        xn = [sb(f"xn{s}", [P, NT, P]) for s in range(LANES)]
        xT = [sb(f"xT{s}", [P, N]) for s in range(LANES)]
        U = [sb(f"U{s}", [P, 2, N]) for s in range(LANES)]
        qs = [sb(f"qs{s}", [P, 4, N], F16) for s in range(LANES)]
        ks = [sb(f"ks{s}", [P, 4, N], F16) for s in range(LANES)]
        vals = [sb(f"vals{s}", [P, NT, P]) for s in range(LANES)]
        tmp = sb("tmp", [P, NT, P])
        rexp = sb("rexp", [P, NT, P])
        hilo = sb("hilo", [P, 2, 2, N], F16)
        identf = sb("identf", [P, P])
        identb = sb("identb", [P, P], BF16)
        ones = sb("ones", [P, P])
        selD = sb("selD", [P, 1])
        mhalf = sb("mhalf", [P, NT])
        wcat = [sb(f"wcat{l}", [P, P + HEADS[l]]) for l in range(2)]
        wsd = [sb(f"wsd{l}", [P, 2 * HEADS[l]]) for l in range(2)]
        woutp = sb("woutp", [P, 2, P])
        wt = {(l, n): sb(f"w{n}T{l}", [P, P]) for l in (2, 3) for n in "qkvo"}
        bcol = {(l, n): sb(f"b{n}{l}", [P, 1]) for l in (2, 3) for n in "qk"}
        bvB = {l: sb(f"bv{l}", [P, P]) for l in (2, 3)}
        bo = {l: sb(f"bo{l}", [1, P]) for l in (2, 3)}
        gammaB = sb("gammaB", [P, P])
        betaB = sb("betaB", [P, P])
        mx = sb("mx", [16, 1])
        diag = sb("diag", [16, 16])
        tops = sb("tops", [P, 16])
        tau = sb("tau", [P, 8])
        rbias = [sb(f"rbias{s}", [P, 8]) for s in range(LANES)]
        kap = [sb(f"kap{s}", [P, 8]) for s in range(LANES)]
        nkap = [sb(f"nkap{s}", [P, 8]) for s in range(LANES)]
        wj = [sb(f"wj{s}", [P, NT, 8]) for s in range(LANES)]
        dm = sb("dm", [P, 4, 8])
        gj = sb("gj", [P, 4, 8])
        gcol = [sb(f"gcol{s}", [P, NT, 32]) for s in range(LANES)]
        rn = sb("rn", [P, 64])
        stats = sb("stats", [P, NT, 6])
        mv = sb("mv", [P, NT, 2])
        veps = sb("veps", [P, NT])
        rstd = sb("rstd", [P, NT])
        mpart = sb("mpart", [P, 32, 2])
        mcol = sb("mcol", [P, 32])
        mrow = sb("mrow", [32, P], F16)
        betac = sb("betac", [P, 4])
        psS = ps("psS", [P, 2, N])
        psU = ps("psU", [P, 2, HALF])
        psX = ps("psX", [P, N])

        vpad = [qs[s][:, :, :].bitcast(F32).rearrange("p a (b h f) -> p (a b) h f", h=8, f=32)
                for s in range(LANES)]

        ring_tile = [ring[:, i, :] for i in range(RING)]
        for s in range(LANES):
            ring_tile += [ks[s][:, 2 * i:2 * i + 2, :].rearrange("p a n -> p (a n)").bitcast(F32) for i in range(2)]
        rho_buf = [rho[:, i, :] for i in range(4)]
        rho_buf += [hilo[:, i, :, :].rearrange("p a n -> p (a n)").bitcast(F32) for i in range(2)]

        chunk = rho[:, 1, :].rearrange("p (b n) -> p b n", b=2)
        rden = rho[:, 2, :].rearrange("p (b n) -> p b n", b=2)
        den_log = rho[:, 3, :].rearrange("p (b n) -> p b n", b=2)

        tile_sum = [[rho[:, 2 * half + p, :] for p in range(2)] for half in range(2)]

        s_x_in = [sem(f"x_in{s}") for s in range(LANES)]
        s_zeroed = sem("vpad_zeroed")
        s_ones_row = sem("ones_row_ready")
        s_xw = sem("psX_written")
        s_xr = sem("psX_read")
        s_diag = sem("diag_ready")
        s_tau = sem("tau_ready")
        s_kap = sem("kappa_ready")
        s_nkap = sem("minus_kappa_ready")
        s_dm = sem("dst_minus_top_ready")
        s_wj = sem("w_and_g_ready")
        s_vals = sem("values_ready")
        s_norm = sem("sums_normalised")
        s_veps = sem("variance_ready")
        s_rstd = sem("rstd_ready")
        s_xn = sem("xn_ready")
        s_xT = sem("xT_ready")
        s_hi = sem("qk_full_and_hi_ready")
        s_lo = sem("qk_lo_ready")
        s_stack = {(l, s): sem(f"stacked{l}{s}") for l in (2, 3) for s in range(LANES)}
        s_mcol = sem("max_columns_ready")
        s_mrow = sem("max_rows_ready")
        s_rho_ps = sem("rho_in_psum")
        s_rho = sem("rho_ready")
        s_scores = sem("scores_ready")
        s_filled = sem("tile_filled")
        s_finished = sem("tile_finished")
        s_used = sem("tile_group_used")
        s_evac = sem("sums_out_of_psum")
        s_chain = sem("vector_chain")
        s_achain = sem("scalar_chain")
        s_den = sem("denominators_ready")
        s_rden = sem("chunk_reciprocals_ready")
        s_scaled = sem("chunk_normalised")
        s_added = sem("chunk_added")
        s_tsum = (sem("tile_added_heads_01"), sem("tile_added_heads_23"))
        s_dsum = sem("row_sums_ready")
        s_out = sem("stored")
        s_done = {e: sem(f"{e}_at_end") for e in ("pe", "act", "dve", "pool")}
        s_go = sem("pair_done", looped=False)
        s_load = sem("weights_loaded", looped=False)
        s_adj = sem("adj_loaded", looped=False)
        s_adjf = sem("adj_as_float", looped=False)
        s_adjT = sem("adj_transposed", looped=False)
        s_adjr = sem("adj_T_out", looped=False)
        s_ln = sem("log_ready", looped=False)
        s_pw = sem("power_ready", looped=False)
        s_edge = sem("edge_ready", looped=False)
        s_id = sem("identity_ready", looped=False)
        s_ones = sem("ones_ready", looped=False)
        s_wT = sem("weight_transposed", looped=False)
        s_wTr = sem("weight_T_out", looped=False)
        s_wpad = sem("wout_padded", looped=False)
        s_b = sem("beta_ready", looped=False)
        s_vset = sem("vector_setup_chain", looped=False)
        s_aset = sem("scalar_setup_chain", looped=False)
        s_setup = sem("setup_done", looped=False)

        adj_i = ring[:, 0:NT, :].bitcast(I32)
        adj_f = ring[:, 0:NT, :]
        stage = [t[:, :, :].bitcast(F32).rearrange("p a n -> p (a n)") for t in (*qs, *ks)]
        adj_eps = [stage[t // 2][:, (t % 2) * N:(t % 2 + 1) * N] for t in range(NT)]
        raw = {("o", 0): rho[:, 0, 0:P]}
        for i, key in enumerate([(n, l) for l in (2, 3) for n in "qkvo"]):
            raw[key] = rho[:, 1, i * P:(i + 1) * P]
        wpad = rho[:, 0, 256:512].rearrange("p (g q r) -> p g q r", g=2, q=4)
        a_row = {0: rho[:, 2, 0:256], 1: rho[:, 2, 256:512]}
        prod = rho[:, 3, 0:P]
        WEIGHTS = [("q", 2), ("k", 2), ("v", 2), ("o", 2), ("q", 3), ("k", 3), ("v", 3), ("o", 3)]

        def lane_of(k):
            return k % LANES

        def due(t, tiles, k):
            weights = [stage_weight(k, name) for name in side_uses(k)]
            return sum(sum(weights[:i]) * tiles < t * sum(weights) for i in range(len(weights)))

        def due_reader(t, tiles, k, engine):
            group, lag = (4, 1, 2, 2)[k // LANES], LAG[engine][k]
            return due(max(0, t // group * group - lag), tiles, k)

        def chunks_before_norm(k):
            uses, tiles = side_uses(k), 4 * NT
            n = next(n for n in range(tiles) if due_reader(n + 1, tiles, k, "dve") > uses.index("out"))
            return (n - 1) // 2 if n >= 3 else 0

        def units_before_norm(k):
            uses, tiles = side_uses(k), 4 * NT
            return next(n + 1 for n in range(tiles) if due_reader(n + 1, tiles, k, "dve") > uses.index("out")) // 2

        def adds_pair(k, n):
            return k == 3 * LANES and n >= PAIR_FROM

        def add_tile(engine, vector, p, k, n):
            half, jt = n // NT, n % NT
            if jt == 0:
                return
            done = accumulated0(k) + (NT - 1) * half + jt - 1
            engine.wait_ge(s_filled, filled0(k) + 2 * n + p + 1)
            if jt > 1:
                engine.wait_ge(s_tsum[p], done)
            elif k == PHASES - 1:
                engine.wait_ge(s_dsum, half + 1)
            t = tile0[k] + 2 * n + p
            total = tile_sum[half][p]
            first = ring_tile[slot_of[t - 2]] if jt == 1 else total
            vector.tensor_tensor(total, first, ring_tile[slot_of[t]], ALU.add).then_inc(s_tsum[p], 1)

        block = ctx.enter_context(nc.Block())

        @block.sync
        def _(sp):
            loads = [
                (wcat[0][:, 0:P].rearrange("p (h f) -> p h f", h=8), w0.rearrange("h d f -> d h f")),
                (wcat[1][:, 0:P], w1),
                (a_row[0][:, 0:P], a0s.rearrange("(o h) f -> o (h f)", o=1).broadcast_to([P, P])),
                (a_row[0][:, P:2 * P], a0d.rearrange("(o h) f -> o (h f)", o=1).broadcast_to([P, P])),
                (a_row[1], a1.rearrange("n o -> o n").broadcast_to([P, 2 * P])),
                (raw["o", 0], wo0),
                (betac[:, 0:1], beta0.broadcast_to([P, 1])),
                (gammaB[:, :], gamma2.rearrange("(o n) -> o n", o=1).broadcast_to([P, P])),
                (betaB[:, :], beta2.rearrange("(o n) -> o n", o=1).broadcast_to([P, P])),
            ]
            for l, w, b in ((2, w2, b2), (3, w3, b3)):
                loads += [(raw[n, l], w[n]) for n in "qkvo"]
                loads += [(bcol[l, n][:, :], b[n].rearrange("(p o) -> p o", o=1)) for n in "qk"]
                loads += [(bvB[l][:, :], b["v"].rearrange("(o n) -> o n", o=1).broadcast_to([P, P])),
                          (bo[l][:, :], b["o"].rearrange("(o n) -> o n", o=1))]
            for dst, src in loads:
                sp.dma_start(dst, src).then_inc(s_load, 16)
            assert len(loads) == N_LOADS
            for t in range(NT):
                sp.dma_start(adj_i[:, t, :], adj[t * P:(t + 1) * P, :]).then_inc(s_adj, 16)

            with sp.Fori(0, PAIRS) as pair:
                for s in range(LANES):
                    sp.dma_start(xn[s][:, :, :], x[LANES * pair + s, :, :].rearrange("(t p) d -> p t d", p=P))\
                      .then_inc(s_x_in[s], 16)
                for k in range(2 * LANES, PHASES):
                    l, s = k // LANES, lane_of(k)
                    if l == 3:
                        sp.wait_ge(s_used, group0[k - LANES + 1])
                    for m, (dst, parts) in enumerate(((qs[s], (0, 0, 1)), (ks[s], (0, 1, 0)))):
                        sp.wait_ge(s_hi, 2 * (k - 4) + m + 1)
                        sp.wait_ge(s_lo, 2 * (k - 4) + m + 1)
                        for h in range(4):
                            for r, part in enumerate(parts):
                                sp.dma_start(dst[r * HD:(r + 1) * HD, h, :],
                                             hilo[h * HD:(h + 1) * HD, m, part, :]).then_inc(s_stack[l, s], 16)
                    if l == 3:
                        sp.wait_ge(s_mrow, k - 6 + 1)
                        sp.dma_start(qs[s][SPLIT_ROWS:SPLIT_ROWS + 1, :, :].rearrange("p h (t i) -> p (h t) i", i=P),
                                     mrow[:, :]).then_inc(s_stack[l, s], 16)
                for s in range(LANES):
                    sp.wait_ge(s_xn, 4 * LANES - 1 + s)
                    sp.dma_start(out[LANES * pair + s, :, :].rearrange("(t p) d -> p t d", p=P), xn[s][:, :, :])\
                      .then_inc(s_out, 16)
                sp.wait_ge(s_out, 16 * LANES)
                for e in s_done.values():
                    sp.wait_ge(e, 1)
                for q in all_sems:
                    sp.sem_clear(q)
                sp.sem_inc(s_go, 1)

        @block.gpsimd
        def _(pool):
            nc.gpsimd.memset(ones[:, :], 1.0).then_inc(s_ones, 1)
            nc.gpsimd.memset(mhalf[:, :], -0.5).then_inc(s_ones, 1)
            nc.gpsimd.memset(identf[:, :], 0.0).then_inc(s_id, 1)
            pool.wait_ge(s_id, 1)
            nc.gpsimd.affine_select(out=identf[:, :], in_=identf[:, :], compare_op=ALU.not_equal, fill=1.0,
                                    base=0, pattern=[[-1, P]], channel_multiplier=1).then_inc(s_id, 1)
            pool.wait_ge(s_id, 2)
            nc.gpsimd.tensor_copy(identb[:, :], identf[:, :]).then_inc(s_id, 1)
            pool.wait_ge(s_setup, 1)

            with pool.Fori(0, PAIRS) as pair:
                for s in range(LANES):
                    nc.gpsimd.memset(vpad[s], 0.0).then_inc(s_zeroed, 1)
                    pool.wait_ge(s_zeroed, s + 1)
                norms = 0

                def rstds(count):
                    nonlocal norms
                    for _ in range(count):
                        norms += 1
                        pool.wait_ge(s_veps, norms)
                        nc.gpsimd.tensor_tensor(rstd[:, :], veps[:, :], mhalf[:, :], ALU.pow).then_inc(s_rstd, 1)

                for k in range(PHASES):
                    l, s = k // LANES, lane_of(k)
                    if k == LANES:
                        pool.wait_ge(s_used, group0[LANES])
                        for i in range(LANES):
                            nc.gpsimd.memset(ks[i][SPLIT_ROWS:SPLIT_ROWS + 1, :, :], 1.0).then_inc(s_ones_row, 1)
                            pool.wait_ge(s_ones_row, i + 1)
                    norms_in_side = 0 if k == 0 else 2 if (k - 1) // LANES == 2 else 1
                    if l == 2:
                        n_added = added0(k)
                        for n in range(2 * NT):
                            half = n // NT
                            if n == chunks_before_norm(k):
                                rstds(norms_in_side)
                            if n % NT:
                                pool.wait_ge(s_scaled, chunks0(k) + n + 1)
                                if n_added:
                                    pool.wait_ge(s_added, n_added)
                                part = U[s][:, 0, half * HALF:(half + 1) * HALF]
                                nc.gpsimd.tensor_tensor(part, part, chunk[:, n % 2, :], ALU.add).then_inc(s_added, 1)
                                n_added += 1
                    elif l == 3:
                        if k == 3 * LANES:
                            pool.wait_ge(s_scaled, chunks0(k))
                            pool.wait_ge(s_added, added0(k))
                        for n in range(2 * NT):
                            if n == units_before_norm(k):
                                rstds(norms_in_side)
                            for p in range(1 + adds_pair(k, n)):
                                add_tile(pool, nc.gpsimd, p, k, n)
                        if units_before_norm(k) >= 2 * NT:
                            rstds(norms_in_side)
                    else:
                        rstds(norms_in_side)
                rstds(1)
                pool.sem_inc(s_done["pool"], 1)
                pool.wait_ge(s_go, pair + 1)

        @block.scalar
        def _(act):
            link_n = [0]

            def link(ins):
                link_n[0] += 1
                ins.then_inc(s_achain, 1)
                act.wait_ge(s_achain, link_n[0])

            act.wait_ge(s_load, 16 * N_LOADS)
            act.wait_ge(s_b, 1)
            act.wait_ge(s_ones, 2)
            nc.scalar.activation(betac[:, 2:3], betac[:, 1:2], ACT.Exp).then_inc(s_aset, 1)
            act.wait_ge(s_aset, 1)
            nc.scalar.activation(betac[:, 3:4], betac[:, 2:3], ACT.Ln, bias=ones[:, 0:1]).then_inc(s_aset, 1)
            for t in range(NT):
                act.wait_ge(s_adjr, t + 1)
                nc.scalar.activation(edge[:, t, :], adj_eps[t], ACT.Ln).then_inc(s_ln, 1)
            act.wait_ge(s_b, 2)
            act.wait_ge(s_ln, NT)
            for t in range(NT):
                nc.scalar.activation(edge[:, t, :], edge[:, t, :], ACT.Exp, scale=betac[:, 1:2]).then_inc(s_pw, 1)
            act.wait_ge(s_setup, 1)

            def gat_rho(k, h):
                l, s = k // LANES, lane_of(k)
                act.wait_ge(s_rho_ps, rho0(k) + h + 1)
                if h >= RHOS:
                    act.wait_ge(s_filled, filled0(k) + 4 * NT)
                elif k >= 1:
                    act.wait_ge(s_filled, filled0(k) - (4 * NT if k <= LANES and h < 2 else 0))
                    if k - 1 >= LANES:
                        act.wait_ge(s_finished, finished0(k))
                nc.scalar.activation(rho_buf[rho_at(k, h)], psS[:, (h + l) % 2, :], ACT.Exp,
                                     bias=rbias[s][:, h:h + 1], scale=1.0 - SLOPE[l]).then_inc(s_rho, 1)

            def side(k):
                for name in side_uses(k):
                    m = x_index.get((k, name))
                    s = lane_of(k + 1)
                    l = (k + 1) // LANES
                    n_gat = k + 1
                    if name == "xT":
                        act.wait_ge(s_xw, m + 1)
                        nc.scalar.activation(xT[s][:, :], psX[:, :], ACT.Copy).then_inc(s_xr, 1)
                    elif name == "top_bc":
                        act.wait_ge(s_tau, n_gat + 1)
                        nc.scalar.activation(kap[s][:, 0:HEADS[l]], tau[:, 0:HEADS[l]], ACT.Exp, scale=-1.0)\
                            .then_inc(s_kap, 1)
                    elif name in ("values0", "values1"):
                        half = int(name[-1])
                        H = HEADS[l]
                        act.wait_ge(s_dm, 2 * n_gat + half + 1)
                        nc.scalar.activation(wj[s][:, 4 * half:4 * half + 4, 0:H], dm[:, :, 0:H], ACT.Exp,
                                             scale=1.0 - SLOPE[l])
                        nc.scalar.activation(gj[:, :, 0:H], dm[:, :, 0:H], ACT.Exp, scale=SLOPE[l]).then_inc(s_wj, 1)
                    elif name in ("q", "k"):
                        q = name == "q"
                        act.wait_ge(s_xw, m + 1)
                        i = 2 * (k + 1 - 4) + (not q)
                        if i >= 1:
                            act.wait_ge(s_lo, i)
                        if i >= 2:
                            j = i // 2 - 1
                            act.wait_ge(s_stack[2 + j // LANES, j % LANES], 24 * 16)
                        nc.scalar.activation(tmp[:, :, :].rearrange("p a b -> p (a b)"), psX[:, :], ACT.Identity,
                                             bias=bcol[l, name][:, :], scale=QSCALE if q else 1.0).then_inc(s_xr, 1)
                        act.wait_ge(s_xr, m + 1)
                        nc.scalar.activation(hilo[:, 1 - q, 0, :], tmp[:, :, :].rearrange("p a b -> p (a b)"),
                                             ACT.Copy).then_inc(s_hi, 1)
                    elif name == "max_rows":
                        act.wait_ge(s_xw, m + 1)
                        nc.scalar.activation(mrow[:, :], psX[0:32, 0:P], ACT.Copy, scale=-1.0).then_inc(s_mrow, 1)
                        act.wait_ge(s_mrow, k + 1 - 6 + 1)
                        act.sem_inc(s_xr, 1)
                    yield

            def free_slot(t):
                if tile_before[t] is not None:
                    b = tile_before[t]
                    act.wait_ge(s_used, group_of[b] + 1)
                    if b >= tile0[3 * LANES]:
                        k, n = 3 * LANES + (b - tile0[3 * LANES]) // (4 * NT), (b - tile0[3 * LANES]) % (4 * NT)
                        half, jt = n // (2 * NT), n // 2 % NT
                        act.wait_ge(s_tsum[n % 2], accumulated0(k) + (NT - 1) * half + max(jt, 1))

            def gat_fill(k, n):
                s, t = lane_of(k), tile0[k] + n
                h, jt = n // (4 * NT) * 4 + n % 4, n % (4 * NT) // 4
                free_slot(t)
                act.wait_ge(s_rho, rho0(k) + h + 1)
                nc.scalar.activation(ring_tile[slot_of[t]], rho_buf[rho_at(k, h)], ACT.Relu,
                                     bias=nkap[s][:, h:h + 1], scale=wj[s][:, jt, h:h + 1]).then_inc(s_filled, 1)

            def gat_start(k):
                act.wait_ge(s_nkap, k + 1)
                act.wait_ge(s_wj, 2 * (k + 1))
                if k < LANES:
                    for h in range(0 if k == 0 else 2, 4):
                        gat_rho(k, h)
                    for n in range(4):
                        gat_fill(k, n)
                elif k > LANES:
                    gat_rho(k, 0)

            def gat_sums_out(k, g):
                act.wait_ge(s_used, group0[k] + NT * (g + 1))
                nc.scalar.activation(U[lane_of(k)][:, g, :], psU[:, :, :].rearrange("p a b -> p (a b)"),
                                     ACT.Copy).then_inc(s_evac, 1)

            with act.Fori(0, PAIRS) as pair:
                link_n[0] = 0
                for _ in side(-1):
                    pass
                for k in range(PHASES):
                    l, s = k // LANES, lane_of(k)
                    stages = side(k)
                    done = 0
                    tiles = {0: 8 * NT, 1: NT, 2: 4 * NT, 3: 4 * NT}[l]

                    def advance(t):
                        nonlocal done
                        while done < due_reader(t, tiles, k, "act"):
                            next(stages)
                            done += 1

                    if l == 0:
                        if k == 0:
                            gat_start(k)
                        for n in range(4, 8 * NT):
                            if n in (8, 12):
                                gat_rho(k, 4 + (n == 12))
                            if n == 4 * NT:
                                gat_rho(k, 6)
                                gat_rho(k, 7)
                            if n == 7 * NT:
                                act.wait_ge(s_tau, k + 2)
                                for h in range(2 if k + 1 < LANES else 1):
                                    gat_rho(k + 1, h)
                            gat_fill(k, n)
                            if n == 4 * NT + 3:
                                gat_sums_out(k, 0)
                            advance(n + 1)
                        for _ in stages:
                            pass
                        gat_start(k + 1)
                        gat_sums_out(k, 1)
                    elif l == 1:
                        if k > LANES:
                            gat_start(k)
                        for n in range(NT):
                            advance(n + 1)
                        act.wait_ge(s_used, group0[k] + NT)
                        nc.scalar.activation(U[s][:, 0, :], psU[:, :, :].rearrange("p a b -> p (a b)"),
                                             ACT.Copy).then_inc(s_evac, 1)
                        nc.scalar.activation(U[s][:, 1, :], psS[:, 0, :], ACT.Copy).then_inc(s_evac, 1)
                    else:
                        def reciprocals(n):
                            i = chunks0(k) + n
                            act.wait_ge(s_den, i + 1)
                            if i >= 2:
                                act.wait_ge(s_rden, i - 1)
                            nc.scalar.activation(den_log[:, n % 2, :], psU[:, 1, :], ACT.Ln).then_inc(s_evac, 1)
                            act.wait_ge(s_evac, evac0(k) + n + 1)
                            if i >= 2:
                                act.wait_ge(s_scaled, i - 1)
                            nc.scalar.activation(rden[:, n % 2, :], den_log[:, n % 2, :], ACT.Exp, scale=-1.0).then_inc(s_rden, 1)

                        def evacuate(half, bank):
                            if bank == 0:
                                act.wait_ge(s_used, group0[k] + NT * (half + 1))
                            else:
                                act.wait_ge(s_dsum, 2 * (k - 3 * LANES) + half + 1)
                            nc.scalar.activation(U[s][:, bank, half * HALF:(half + 1) * HALF], psU[:, bank, :],
                                                 ACT.Copy).then_inc(s_evac, 1)

                        for n in range(2 * NT):
                            for p in range(2):
                                t = tile0[k] + 2 * n + p
                                act.wait_ge(s_scores, 4 * NT * (k - 4) + 2 * n + p + 1)
                                free_slot(t)
                                nc.scalar.activation(ring_tile[slot_of[t]], psS[:, p, :], ACT.Exp).then_inc(s_filled, 1)
                                if l == 2 and n >= 1 and p == 1:
                                    reciprocals(n - 1)
                                if l == 3 and n in (NT, NT + 1) and p == 1:
                                    evacuate(0, n - NT)
                                advance(2 * n + p + 1)
                        if l == 2:
                            reciprocals(2 * NT - 1)
                        else:
                            evacuate(1, 0)
                            evacuate(1, 1)
                    for _ in stages:
                        pass
                for _ in side(PHASES):
                    pass
                act.sem_inc(s_done["act"], 1)
                act.wait_ge(s_go, pair + 1)

        @block.vector
        def _(dve):
            link_n = [0]
            chain = [s_vset]

            def link(ins):
                link_n[0] += 1
                ins.then_inc(chain[0], 1)
                dve.wait_ge(chain[0], link_n[0])

            dve.wait_ge(s_load, 16 * N_LOADS)
            link(nc.vector.tensor_scalar(betac[:, 1:2], betac[:, 0:1], -1.0, None, ALU.mult))
            nc.vector.tensor_tensor(betac[:, 1:2], betac[:, 0:1], betac[:, 1:2], ALU.min).then_inc(s_b, 1)
            dve.wait_ge(s_aset, 2)
            nc.vector.scalar_tensor_tensor(betac[:, 1:2], betac[:, 0:1], 0.0, betac[:, 3:4], ALU.max, ALU.add)\
                .then_inc(s_b, 1)
            for l in range(2):
                H = HEADS[l]
                for side_ in range(2):
                    link(nc.vector.tensor_tensor(prod, wcat[l][:, 0:P], a_row[l][:, side_ * P:(side_ + 1) * P], ALU.mult))
                    link(nc.vector.tensor_reduce(wsd[l][:, side_ * H:(side_ + 1) * H],
                                                 prod.rearrange("p (h f) -> p h f", h=H), AX.X, ALU.add))
                link(nc.vector.tensor_copy(wcat[l][:, P:P + H], wsd[l][:, H:2 * H]))
            link(nc.vector.memset(rho[:, 0, 256:512], 0.0))
            nc.vector.tensor_copy(wpad[:, :, :, 0:16],
                                  raw["o", 0].rearrange("p (g q r) -> p g q r", g=2, q=4)).then_inc(s_wpad, 1)
            dve.wait_ge(s_id, 3)
            link(nc.vector.tensor_reduce(selD[:, :], identf[:, 0:P:32], AX.X, ALU.add))
            dve.wait_ge(s_adj, 16 * NT)
            for it in range(NT):
                nc.vector.tensor_copy(adj_f[:, it, :], adj_i[:, it, :]).then_inc(s_adjf, 1)
            for jt in range(NT):
                dve.wait_ge(s_adjT, jt + 1)
                nc.vector.tensor_scalar(absent[:, jt, :], psS[:, jt % 2, :], 0.0, ABSENT, ALU.is_equal, ALU.mult)
                nc.vector.tensor_scalar(adj_eps[jt], psS[:, jt % 2, :], 0.0, EPS_LOG, ALU.max, ALU.add)\
                    .then_inc(s_adjr, 1)
            for i, (n, l) in enumerate(WEIGHTS):
                dve.wait_ge(s_wT, i + 1)
                nc.vector.tensor_copy(wt[l, n][:, :], psX[:, (i % 2) * HALF:(i % 2) * HALF + P]).then_inc(s_wTr, 1)
            for g in range(2):
                i = len(WEIGHTS) + g
                dve.wait_ge(s_wT, i + 1)
                nc.vector.tensor_copy(woutp[:, g, :], psX[:, (i % 2) * HALF:(i % 2) * HALF + P]).then_inc(s_wTr, 1)
            for l in (2, 3):
                link(nc.vector.tensor_scalar(bcol[l, "q"][:, :], bcol[l, "q"][:, :], QSCALE, None, ALU.mult))
            for t in range(NT):
                dve.wait_ge(s_pw, t + 1)
                link(nc.vector.scalar_tensor_tensor(edge[:, t, :], adj_eps[t], EPS_LOG, edge[:, t, :],
                                                    ALU.is_gt, ALU.mult))
            nc.vector.memset(veps[:, :], 0.0).then_inc(s_setup, 1)
            chain[0] = s_chain

            def gat_prologue(k, name, m):
                l, s = (k + 1) // LANES, lane_of(k + 1)
                n, H, lam = k + 1, HEADS[l], 1.0 - SLOPE[l]
                if name == "tops":
                    dve.wait_ge(s_xw, m + 1)
                    nc.vector.tensor_reduce(mx[0:2 * H, :], psX[0:2 * H, :], AX.X, ALU.max).then_inc(s_xr, 1)
                    dve.wait_ge(s_xr, m + 1)
                    nc.vector.tensor_scalar(diag[0:2 * H, 0:2 * H], identf[0:2 * H, 0:2 * H], mx[0:2 * H, :], None,
                                            ALU.mult).then_inc(s_diag, 1)
                elif name == "top_bc":
                    dve.wait_ge(s_xw, m + 1)
                    nc.vector.tensor_copy(tops[:, 0:2 * H], psX[:, 0:2 * H]).then_inc(s_xr, 1)
                    dve.wait_ge(s_xr, m + 1)
                    link(nc.vector.tensor_tensor(tau[:, 0:H], tops[:, 0:H], tops[:, H:2 * H], ALU.add))
                    link(nc.vector.tensor_scalar(tau[:, 0:H], tau[:, 0:H], lam, -TAU_START, ALU.mult, ALU.add))
                    link(nc.vector.tensor_scalar(tau[:, 0:H], tau[:, 0:H], 0.0, None, ALU.max))
                    nc.vector.scalar_tensor_tensor(rbias[s][:, 0:H], tops[:, H:2 * H], lam, tau[:, 0:H],
                                                   ALU.mult, ALU.subtract).then_inc(s_tau, 1)
                elif name == "kappa":
                    dve.wait_ge(s_kap, n + 1)
                    nc.vector.tensor_scalar(nkap[s][:, 0:H], kap[s][:, 0:H], -1.0, None, ALU.mult).then_inc(s_nkap, 1)
                elif name in ("values0", "values1"):
                    half = int(name[-1])
                    dve.wait_ge(s_xw, m + 1)
                    if 2 * n + half >= 1:
                        dve.wait_ge(s_wj, 2 * n + half)
                    v = psX[:, :].rearrange("p (t c) -> p t c", c=2 * P)
                    nc.vector.tensor_tensor(dm[:, :, 0:H], v[:, :, P:P + H],
                                            tops[:, H:2 * H].unsqueeze(1).broadcast_to([P, 4, H]), ALU.subtract)\
                        .then_inc(s_dm, 1)
                else:
                    half = int(name[-1])
                    jts = slice(4 * half, 4 * half + 4)
                    v = psX[:, :].rearrange("p (t c) -> p t c", c=2 * P)
                    dve.wait_ge(s_wj, 2 * n + half + 1)
                    if l == 0:
                        if half == 0:
                            dve.wait_ge(s_zeroed, s + 1)
                        nc.vector.tensor_copy(vpad[s][:, jts, :, 16:17], gj[:, :, 0:H].unsqueeze(3)).then_inc(s_vals, 1)
                        nc.vector.tensor_tensor(vpad[s][:, jts, :, 0:16],
                                                v[:, :, 0:P].rearrange("p t (h f) -> p t h f", h=H),
                                                gj[:, :, 0:H].unsqueeze(3).broadcast_to([P, 4, H, 16]), ALU.mult)\
                            .then_inc(s_xr, 1)
                    else:
                        nc.vector.tensor_copy(gcol[s][:, jts, :], gj[:, :, 0:1].broadcast_to([P, 4, 32]))\
                            .then_inc(s_vals, 1)
                        nc.vector.tensor_tensor(vals[s][:, jts, :], v[:, :, 0:P],
                                                gj[:, :, 0:1].broadcast_to([P, 4, P]), ALU.mult).then_inc(s_xr, 1)

            norms = [0]

            def normalise(dst, src):
                for t in range(NT):
                    ins = nc.vector.bn_stats(stats[:, t, :], src[:, t, :])
                link(ins)
                for t in range(NT):
                    ins = nc.vector.bn_aggr(mv[:, t, :], stats[:, t, :])
                link(ins)
                norms[0] += 1
                nc.vector.tensor_scalar(veps[:, :], mv[:, :, 1], EPS_LN, None, ALU.add).then_inc(s_veps, 1)
                dve.wait_ge(s_rstd, norms[0])
                for t in range(NT):
                    ins = nc.vector.tensor_scalar(dst[:, t, :], src[:, t, :], mv[:, t, 0:1], rstd[:, t:t + 1],
                                                  ALU.subtract, ALU.mult)
                return ins

            def epilogue(k, name, m):
                l, s = (k - 1) // LANES, lane_of(k - 1)
                ps3 = psX[:, :].rearrange("p (t d) -> p t d", d=P)
                if uses_psX(name):
                    dve.wait_ge(s_xw, m + 1)

                if name == "norm":
                    dve.wait_ge(s_evac, evac0(k))
                    blocks = N // 32
                    work = [tmp, rexp][:2 if l == 0 else 1]
                    flat = [w[:, :, :].rearrange("p a b -> p (a b)") for w in work]
                    for g, w in enumerate(flat):
                        ins = nc.vector.transpose(w, U[s][:, g if l == 0 else 1, :])
                    link(ins)
                    for g, w in enumerate(flat):
                        sums, r = w.rearrange("p (b c) -> p b c", c=32)[:, :, 16], rn[:, g * blocks:(g + 1) * blocks]
                        if l == 3:
                            link(nc.vector.tensor_scalar(r, sums, 1e-37, None, ALU.max))
                            sums = r
                        ins = nc.vector.reciprocal(r, sums)
                    link(ins)
                    for g, w in enumerate(flat):
                        ins = nc.vector.transpose(w, rn[:, g * blocks:(g + 1) * blocks].unsqueeze(2)
                                                  .broadcast_to([P, blocks, 32]))
                    link(ins)
                    for g, w in enumerate(flat):
                        ins = nc.vector.tensor_tensor(U[s][:, g, :], U[s][:, g, :], w, ALU.mult)
                    ins.then_inc(s_norm, 1)
                elif name == "den":
                    nc.vector.reciprocal(rn[:, 0:NT], psX[:, 0:NT]).then_inc(s_xr, 1)
                    dve.wait_ge(s_xr, m + 1)
                elif name == "out":
                    if l == 1:
                        nc.vector.scalar_tensor_tensor(tmp[:, :, :], ps3, 0.0,
                                                       rn[:, 0:NT].unsqueeze(2).broadcast_to([P, NT, P]),
                                                       ALU.max, ALU.mult).then_inc(s_xr, 1)
                        dve.wait_ge(s_xr, m + 1)
                        link(nc.vector.tensor_tensor(tmp[:, :, :], tmp[:, :, :], xn[s][:, :, :], ALU.add))
                    else:
                        nc.vector.tensor_tensor(tmp[:, :, :], ps3, xn[s][:, :, :], ALU.add).then_inc(s_xr, 1)
                        dve.wait_ge(s_xr, m + 1)
                    if l == 2:
                        link(normalise(tmp, tmp))
                        link(nc.vector.tensor_tensor(tmp[:, :, :], tmp[:, :, :],
                                                     gammaB[:, :].unsqueeze(1).broadcast_to([P, NT, P]), ALU.mult))
                        link(nc.vector.tensor_tensor(tmp[:, :, :], tmp[:, :, :],
                                                     betaB[:, :].unsqueeze(1).broadcast_to([P, NT, P]), ALU.add))
                        link(nc.vector.tensor_tensor(tmp[:, :, :], tmp[:, :, :], xn[s][:, :, :], ALU.add))
                    normalise(xn[s], tmp).then_inc(s_xn, 1)

            def side(k):
                n_epilogue = len(side_uses(k)) - (len(side_uses(-1)) if k == -1 else 0)
                names = side_uses(k)
                in_epilogue = k >= 1
                for name in names:
                    m = x_index.get((k, name))
                    if name == "xT":
                        in_epilogue = False
                    l, s = (k + 1) // LANES, lane_of(k + 1)
                    if in_epilogue:
                        epilogue(k, name, m)
                    elif name in ("tops", "top_bc", "kappa", "values0", "g0", "values1", "g1"):
                        gat_prologue(k, name, m)
                    elif name in ("q", "k"):
                        q = name == "q"
                        i = 2 * (k + 1 - 4) + (not q)
                        dve.wait_ge(s_hi, i + 1)
                        if i >= 2:
                            j = i // 2 - 1
                            dve.wait_ge(s_stack[2 + j // LANES, j % LANES], 24 * 16)
                        nc.vector.tensor_tensor(hilo[:, 1 - q, 1, :], tmp[:, :, :].rearrange("p a b -> p (a b)"),
                                                hilo[:, 1 - q, 0, :], ALU.subtract).then_inc(s_lo, 1)
                    elif name == "v":
                        dve.wait_ge(s_xw, m + 1)
                        nc.vector.tensor_tensor(vals[s][:, :, :], psX[:, :].rearrange("p (t d) -> p t d", d=P),
                                                bvB[l][:, :].unsqueeze(1).broadcast_to([P, NT, P]), ALU.add)\
                            .then_inc(s_xr, 1)
                    elif name.startswith("max") and name != "max_rows":
                        i = int(name[3:])
                        dve.wait_ge(s_xw, m + 1)
                        nc.vector.tensor_reduce(mpart[:, i // 2, i % 2:i % 2 + 1],
                                                psX[:, (i % 2) * HALF:(i % 2 + 1) * HALF], AX.X, ALU.max)\
                            .then_inc(s_xr, 1)
                        if i == 63:
                            dve.wait_ge(s_xr, m + 1)
                            nc.vector.tensor_reduce(mcol[:, :], mpart[:, :, :], AX.X, ALU.max).then_inc(s_mcol, 1)
                    yield

            def normalise_chunk(k, n):
                s, half, i = lane_of(k), n // NT, chunks0(k) + n
                dve.wait_ge(s_used, group0[k] + n + 1)
                dve.wait_ge(s_rden, i + 1)
                if n >= 2:
                    dve.wait_ge(s_added, added0(k) + sum(1 for j in range(n - 1) if j % NT))
                elif k == 5:
                    dve.wait_ge(s_added, added0(k))
                dst = chunk[:, n % 2, :] if n % NT else U[s][:, 0, half * HALF:(half + 1) * HALF]
                nc.vector.tensor_tensor(dst, psU[:, 0, :], rden[:, n % 2, :], ALU.mult).then_inc(s_scaled, 1)

            with dve.Fori(0, PAIRS) as pair:
                link_n[0] = 0
                norms[0] = 0
                for _ in side(-1):
                    pass
                for k in range(PHASES):
                    l, s = k // LANES, lane_of(k)
                    stages = side(k)
                    done = 0
                    tiles = {0: 8 * NT, 1: NT, 2: 4 * NT, 3: 4 * NT}[l]
                    for n in range(tiles):
                        t = tile0[k] + n
                        slot = ring_tile[slot_of[t]]
                        if l == 0:
                            g, jt, h = n // 32, n % 32 // 4, n // 32 * 4 + n % 4
                            dve.wait_ge(s_filled, filled0(k) + n + 1)
                            nc.vector.scalar_tensor_tensor(slot, slot, kap[s][:, h:h + 1], edge[:, jt, :],
                                                           ALU.add, ALU.mult).then_inc(s_finished, 1)
                        elif l == 1:
                            if n == 0:
                                dve.wait_ge(s_rho, rho0(k) + 1)
                            dve.wait_ge(s_used, group_of[tile_before[t]] + 1)
                            link(nc.vector.tensor_scalar(slot, rho_buf[rho_at(k, 0)], wj[s][:, n, 0:1], kap[s][:, 0:1],
                                                         ALU.mult, ALU.max))
                            nc.vector.scalar_tensor_tensor(slot, absent[:, n, :], 0.0, slot,
                                                           ALU.is_equal, ALU.mult).then_inc(s_finished, 1)
                        elif l == 2:
                            dve.wait_ge(s_filled, filled0(k) + n + 1)
                            nc.vector.tensor_scalar(slot, slot, math.exp(-CLIP), math.exp(CLIP), ALU.max, ALU.min)\
                                .then_inc(s_finished, 1)
                            if n % 2 and n >= 3:
                                normalise_chunk(k, n // 2 - 1)
                        elif n % 2:
                            if n == 1 and k == 3 * LANES:
                                dve.wait_ge(s_rden, chunks0(k))
                                dve.wait_ge(s_added, added0(k))
                            if not adds_pair(k, n // 2):
                                add_tile(dve, nc.vector, 1, k, n // 2)
                        while done < due_reader(n + 1, tiles, k, "dve"):
                            next(stages)
                            done += 1
                    if l == 2:
                        normalise_chunk(k, 2 * NT - 1)
                    for _ in stages:
                        pass
                for _ in side(PHASES):
                    pass
                dve.sem_inc(s_done["dve"], 1)
                dve.wait_ge(s_go, pair + 1)

        @block.tensor
        def _(pe):
            mm = nc.tensor.matmul

            pe.wait_ge(s_id, 3)
            pe.wait_ge(s_adjf, NT)
            for jt in range(NT):
                if jt >= 2:
                    pe.wait_ge(s_adjr, jt - 1)
                for it in range(NT):
                    ins = nc.tensor.transpose(psS[:, jt % 2, it * P:(it + 1) * P],
                                              adj_f[:, it, jt * P:(jt + 1) * P], identf[:, :])
                ins.then_inc(s_adjT, 1)
            pe.wait_ge(s_load, 16 * N_LOADS)
            for i, (n, l) in enumerate(WEIGHTS):
                if i >= 2:
                    pe.wait_ge(s_wTr, i - 1)
                nc.tensor.transpose(psX[:, (i % 2) * HALF:(i % 2) * HALF + P], raw[n, l], identf[:, :]).then_inc(s_wT, 1)
            pe.wait_ge(s_wpad, 1)
            for g in range(2):
                i = len(WEIGHTS) + g
                pe.wait_ge(s_wTr, i - 1)
                nc.tensor.transpose(psX[:, (i % 2) * HALF:(i % 2) * HALF + P],
                                    wpad[:, g, :, :].rearrange("p q r -> p (q r)"), identf[:, :]).then_inc(s_wT, 1)
            pe.wait_ge(s_wTr, len(WEIGHTS) + 2)
            pe.wait_ge(s_setup, 1)

            def side(k):
                in_epilogue = k >= 1
                for name in side_uses(k):
                    if not uses_psX(name):
                        yield
                        continue
                    m = x_index[k, name]
                    if name == "xT":
                        in_epilogue = False
                    j = k - 1 if in_epilogue else k + 1
                    l, s = j // LANES, lane_of(j)
                    turns = name.startswith("max") and name not in ("max0", "max_rows")
                    if m - turns >= 1:
                        pe.wait_ge(s_xr, m - turns)

                    if name == "den":
                        pe.wait_ge(s_evac, evac0(j + 1))
                        for t in range(NT):
                            ins = mm(psX[:, t:t + 1], U[s][:, 1, t * P:(t + 1) * P], selD[:, :],
                                     start=True, stop=True)
                    elif name == "out":
                        if l == 2:
                            pe.wait_ge(s_added, added0(j + 1))
                        if l in (0, 3):
                            pe.wait_ge(s_norm, before(j + 1, (1, 0, 0, 1)))
                        for t in range(NT):
                            o = psX[:, t * P:(t + 1) * P]
                            if l == 0:
                                mm(o, U[s][:, 0, t * P:(t + 1) * P], woutp[:, 0, :], start=True, stop=False)
                                ins = mm(o, U[s][:, 1, t * P:(t + 1) * P], woutp[:, 1, :], start=False, stop=True)
                            elif l == 1:
                                ins = nc.tensor.transpose(o, U[s][:, 0, t * P:(t + 1) * P], identf[:, :])
                            else:
                                mm(o, U[s][:, 0, t * P:(t + 1) * P], wt[l, "o"][:, :], start=True, stop=False)
                                ins = mm(o, ones[0:1, :], bo[l][:, :], start=False, stop=True)
                    elif name == "xT":
                        if l == 0:
                            pe.wait_ge(s_x_in[s], 16)
                        else:
                            pe.wait_ge(s_xn, k)
                        for t in range(NT):
                            ins = nc.tensor.transpose(psX[:, t * P:(t + 1) * P], xn[s][:, t, :], identf[:, :])
                    elif name == "tops":
                        H = HEADS[l]
                        for i in range(2):
                            ins = mm(psX[0:2 * H, i * HALF:(i + 1) * HALF], wsd[l][:, :],
                                     xT[s][:, i * HALF:(i + 1) * HALF], start=True, stop=True)
                    elif name == "top_bc":
                        H = HEADS[l]
                        pe.wait_ge(s_diag, k + 2)
                        ins = mm(psX[:, 0:2 * H], ones[0:2 * H, :], diag[0:2 * H, 0:2 * H], start=True, stop=True)
                    elif name in ("values0", "values1"):
                        for i in range(4):
                            t = 4 * int(name[-1]) + i
                            ins = mm(psX[:, i * 2 * P:i * 2 * P + P + HEADS[l]], xT[s][:, t * P:(t + 1) * P],
                                     wcat[l][:, :], start=True, stop=True)
                    elif name in ("q", "k"):
                        for i in range(2):
                            ins = mm(psX[:, i * HALF:(i + 1) * HALF], wt[l, name][:, :],
                                     xT[s][:, i * HALF:(i + 1) * HALF], start=True, stop=True)
                    elif name == "v":
                        for t in range(NT):
                            ins = mm(psX[:, t * P:(t + 1) * P], xT[s][:, t * P:(t + 1) * P], wt[l, "v"][:, :],
                                     start=True, stop=True)
                    elif name == "max_rows":
                        pe.wait_ge(s_mcol, j - 6 + 1)
                        ins = nc.tensor.transpose(psX[0:32, 0:P], mcol[:, :], identf[:, :])
                    else:
                        i = int(name[3:])
                        if i == 0:
                            pe.wait_ge(s_stack[l, s], 24 * 16)
                        h, t, jh = i // 16, i % 16 // 2, i % 2
                        ins = mm(psX[:, jh * HALF:(jh + 1) * HALF], qs[s][0:SPLIT_ROWS, h, t * P:(t + 1) * P],
                                 ks[s][0:SPLIT_ROWS, h, jh * HALF:(jh + 1) * HALF], start=True, stop=True)
                    ins.then_inc(s_xw, 1)
                    yield

            def rho_rows(k, h):
                l, s = k // LANES, lane_of(k)
                if h == 0:
                    pe.wait_ge(s_xr, x_index[k - 1, "xT"] + 1)
                if rho0(k) + h >= 2:
                    pe.wait_ge(s_rho, rho0(k) + h - (l == 0))
                for i in range(2):
                    ins = mm(psS[:, (h + l) % 2, i * HALF:(i + 1) * HALF],
                             wsd[l][:, h:h + 1].broadcast_to([P, P]), xT[s][:, i * HALF:(i + 1) * HALF],
                             start=True, stop=True)
                ins.then_inc(s_rho_ps, 1)

            with pe.Fori(0, PAIRS) as pair:
                for _ in side(-1):
                    pass
                for k in range(PHASES):
                    l, s = k // LANES, lane_of(k)
                    stages = side(k)
                    done = 0
                    tiles = {0: 8 * NT, 1: NT, 2: 4 * NT, 3: 4 * NT}[l]

                    def advance(t):
                        nonlocal done
                        while done < due(t, tiles, k):
                            next(stages)
                            done += 1

                    if l == 0:
                        if k == 0:
                            for h in range(4):
                                rho_rows(k, h)
                        rho_rows(k, 4)
                        rho_rows(k, 5)
                    if k >= 1:
                        pe.wait_ge(s_evac, evac0(k))
                        pe.wait_ge(s_filled, filled0(k))
                        if l >= 1:
                            pe.wait_ge(s_rho, rho0(k))
                        if chunks0(k):
                            pe.wait_ge(s_scaled, chunks0(k))
                    if l == 0:
                        pe.wait_ge(s_xr, x_index[k - 1, "values1"] + 1)
                        for g in range(2):
                            if g == 1:
                                pe.wait_ge(s_evac, evac0(k) + 1)
                            for jt in range(NT):
                                if g == 0 and jt in (4, 5):
                                    rho_rows(k, 2 + jt)
                                if g == 1 and jt == 3:
                                    for h in range(2 if k + 1 < LANES else 1):
                                        rho_rows(k + 1, h)
                                if g == 1 and jt == 5 and k + 1 < LANES:
                                    rho_rows(k + 1, 2)
                                    rho_rows(k + 1, 3)
                                n = 4 * (g * NT + jt)
                                pe.wait_ge(s_finished, finished0(k) + n + 4)
                                for i in range(2):
                                    for q in range(4):
                                        t = tile0[k] + n + q
                                        ins = mm(psU[q * 32:(q + 1) * 32, i, :], vpad[s][:, jt, 4 * g + q, :],
                                                 ring_tile[slot_of[t]][:, i * HALF:(i + 1) * HALF],
                                                 start=(jt == 0), stop=(jt == NT - 1))
                                ins.then_inc(s_used, 1)
                                advance(n + 4)
                    elif l == 1:
                        if k > LANES:
                            rho_rows(k, 0)
                        pe.wait_ge(s_xr, x_index[k - 1, "values1"] + 1)
                        for jt in range(NT):
                            t = tile0[k] + jt
                            q = jt % 4
                            pe.wait_ge(s_finished, finished0(k) + jt + 1)
                            for i in range(2):
                                tile = ring_tile[slot_of[t]][:, i * HALF:(i + 1) * HALF]
                                mm(psU[:, i, :], vals[s][:, jt, :], tile, start=(jt == 0), stop=(jt == NT - 1))
                                ins = mm(psS[q * 32:(q + 1) * 32, 0, i * HALF:(i + 1) * HALF], gcol[s][:, jt, :], tile,
                                         start=(jt < 4), stop=(jt >= 4))
                            ins.then_inc(s_used, 1)
                            advance(jt + 1)
                    else:
                        rows = SPLIT_ROWS + (l == 3)
                        pe.wait_ge(s_stack[l, s], (24 + (l == 3)) * 16)
                        if l == 3:
                            pe.wait_ge(s_ones_row, s + 1)
                        pe.wait_ge(s_xr, x_index[k - 1, "v"] + 1)

                        points = POINTS[k]

                        def scores(n):
                            half, jt = n // NT, n % NT
                            cols = slice(half * HALF, (half + 1) * HALF)
                            for p in range(2):
                                if n >= 1:
                                    pe.wait_ge(s_filled, filled0(k) + 2 * (n - 1) + p + 1)
                                for i in range(2):
                                    o = psS[:, p, i * HALF:(i + 1) * HALF]
                                    h = 2 * p + i
                                    mm(o, ks[s][0:rows, h, jt * P:(jt + 1) * P], qs[s][0:rows, h, cols],
                                       start=True, stop=False)
                                    ins = mm(o, identb[:, :], absent[:, jt, cols], start=False, stop=True)
                                ins.then_inc(s_scores, 1)
                                if n >= 1 and points > 2 + p:
                                    advance(2 * n - 1.5 + p * 0.5)

                        def sums(n):
                            half, jt = n // NT, n % NT
                            if l == 2 and n >= 1:
                                pe.wait_ge(s_evac, evac0(k) + n)
                            if l == 3 and n == NT:
                                pe.wait_ge(s_evac, evac0(k) + 1)
                            if l == 2:
                                pe.wait_ge(s_finished, finished0(k) + 2 * n + 2)
                            else:
                                pe.wait_ge(s_filled, filled0(k) + 2 * n + 2)
                            for bank in (1, 0) if l == 2 else (0,):
                                if l == 2 and n >= 1 and bank == 0:
                                    pe.wait_ge(s_scaled, chunks0(k) + n)
                                for h in range(4):
                                    t = tile0[k] + 2 * n + h // 2
                                    w = ones[:, 0:HD] if bank else vals[s][:, jt, h * HD:(h + 1) * HD]
                                    ins = mm(psU[h * 32:(h + 1) * 32, bank, :], w,
                                             ring_tile[slot_of[t]][:, (h % 2) * HALF:(h % 2 + 1) * HALF],
                                             start=(l == 2 or jt == 0), stop=(l == 2 or jt == NT - 1))
                                if l == 2 and bank == 1:
                                    ins.then_inc(s_den, 1)
                                if bank == 1 and points > 1:
                                    advance(2 * n + 1.5)
                            ins.then_inc(s_used, 1)

                        def row_sums(half):
                            if half:
                                pe.wait_ge(s_evac, evac0(k) + 2)
                            for p in range(2):
                                pe.wait_ge(s_tsum[p], accumulated0(k) + (NT - 1) * (half + 1))
                            for h in range(4):
                                ins = mm(psU[h * 32:(h + 1) * 32, 1, :], ones[:, 0:HD],
                                         tile_sum[half][h // 2][:, (h % 2) * HALF:(h % 2 + 1) * HALF],
                                         start=True, stop=True)
                            ins.then_inc(s_dsum, 1)

                        scores(0)
                        for n in range(2 * NT):
                            if n + 1 < 2 * NT:
                                scores(n + 1)
                            sums(n)
                            advance(2 * n + 2)
                            if l == 3 and n == NT:
                                row_sums(0)
                        if l == 3:
                            row_sums(1)
                for _ in side(PHASES):
                    pass
                pe.sem_inc(s_done["pe"], 1)
                pe.wait_ge(s_go, pair + 1)


N_LOADS = 9 + 2 * (4 + 2 + 2)

_INS = ['x', 'adj', 'L0_gnn_W', 'L0_gnn_a_src', 'L0_gnn_a_dst', 'L0_gnn_beta_tilde', 'L0_gnn_W_out', 'L1_gnn_W',
        'L1_gnn_a', 'L2_gnn_Wq', 'L2_gnn_bq', 'L2_gnn_Wk', 'L2_gnn_bk', 'L2_gnn_Wv', 'L2_gnn_bv', 'L2_gnn_Wo',
        'L2_gnn_bo', 'L2_gnn_gamma', 'L2_gnn_beta', 'L3_gnn_wq', 'L3_gnn_bq', 'L3_gnn_wk', 'L3_gnn_bk', 'L3_gnn_wv',
        'L3_gnn_bv', 'L3_gnn_wo', 'L3_gnn_bo']


def program(nc, t, out):
    build(nc, t["x"], t["adj"], t["L0_gnn_W"], t["L0_gnn_a_src"], t["L0_gnn_a_dst"], t["L0_gnn_beta_tilde"],
          t["L0_gnn_W_out"], t["L1_gnn_W"], t["L1_gnn_a"],
          {n: t[f"L2_gnn_W{n}"] for n in "qkvo"}, {n: t[f"L2_gnn_b{n}"] for n in "qkvo"},
          t["L2_gnn_gamma"], t["L2_gnn_beta"],
          {n: t[f"L3_gnn_w{n}"] for n in "qkvo"}, {n: t[f"L3_gnn_b{n}"] for n in "qkvo"}, out)


def kernel(**inputs):
    import numpy as _np
    import concourse.bacc as _bacc
    from concourse import mybir as _mybir
    from concourse.bass_utils import run_bass_kernel_spmd as _run

    nc = _bacc.Bacc("TRN2", target_bir_lowering=False, num_devices=1)
    arrays, args = {}, {}
    for name in _INS:
        a = _np.ascontiguousarray(inputs[name])
        if a.ndim == 0:
            a = a.reshape(1, 1)
        arrays[f"in_{name}_dram"] = a
        args[name] = nc.dram_tensor(f"in_{name}_dram", a.shape, _mybir.dt.from_np(a.dtype), kind="ExternalInput").ap()
    out = nc.dram_tensor("out_dram", inputs["x"].shape, _mybir.dt.float32, kind="ExternalOutput").ap()
    program(nc, args, out)
    r = _run(nc, [arrays], core_ids=[0])
    return r.results[0]["out_dram"]
```

```python
import math
from contextlib import ExitStack

import concourse.bass as bass
from concourse import mybir

F32 = mybir.dt.float32
F16 = mybir.dt.float16
BF16 = mybir.dt.bfloat16
I32 = mybir.dt.int32
ALU = mybir.AluOpType
ACT = mybir.ActivationFunctionType
AX = mybir.AxisListType

P = 128
LANES = 2
LAYERS = 4
PHASES = LANES * LAYERS
HALF = 512
EPS_LN = 1e-5
EPS_LOG = 1e-6
ABSENT = -1e30
HEADS = (8, 1, 4, 4)
SLOPE = (0.2, 0.01)
TAU_START = 80.0
CLIP = 10.0
HD = 32
SPLIT_ROWS = 3 * HD
RING = 8
LONG_RING = 12
LAG = {"act": (12, 12, 0, 0, 2, 0, 0, 2), "dve": (4, 8, 2, 2, 2, 0, 0, 0)}
RHOS = 6


def phase_plan(NT):
    groups = {0: [4] * (2 * NT), 1: [4] * (NT // 4), 2: [2] * (2 * NT), 3: [2] * (2 * NT)}
    tile0, group0, group_of = [], [], []
    n_groups = 0
    for k in range(PHASES):
        tile0.append(len(group_of))
        group0.append(n_groups)
        for size in groups[k // LANES]:
            group_of += [n_groups] * size
            n_groups += 1
    return tile0, group0, group_of


def ring_slots(tile0, n_tiles):
    slots, before, last = [], [], {}
    for t in range(n_tiles):
        slot = t % (LONG_RING if t < tile0[LANES] else RING)
        slots.append(slot)
        before.append(last.get(slot))
        last[slot] = t
    return slots, before


def epilogue_of(k):
    return (k - 1) % PHASES


def prologue_of(k):
    return (k + 1) % PHASES


def gat_before(j):
    return LANES * 2 - 1 if j == 0 else j - 1


def side_uses(k):
    uses = []
    if k >= 0:
        layer = epilogue_of(k) // LANES
        uses += {0: ["norm", "out"], 1: ["den", "out"], 2: ["out"], 3: ["norm", "out"]}[layer]
    if k < PHASES:
        layer = prologue_of(k) // LANES
        uses += ["xT"]
        uses += (["tops", "top_bc", "kappa", "values0", "g0", "values1", "g1"] if layer < 2 else ["q", "k", "v"])
        if layer == 3:
            uses += [f"max{n}" for n in range(64)] + ["max_rows"]
    return uses


def uses_psX(name):
    return name not in ("norm", "kappa", "g0", "g1")


WEIGHTS_OF = [
    dict(norm=3, out=10, top_bc=2, kappa=3, values0=5),
    dict(out=10, top_bc=10, values0=7, values1=2, g1=3),
    dict(norm=5, out=10, tops=2, top_bc=2, kappa=7, values0=2),
    dict(xT=2, k=10, v=3),
    dict(den=3, out=25, xT=5, k=25, v=8),
    dict(out=10, k=6, v=16, max_rows=2),
    dict(out=28, k=6, v=24),
    dict(out=17, xT=2, tops=6, top_bc=3, g0=2, values1=5),
]
PAIR_FROM = 8
POINTS = (1, 1, 1, 1, 1, 4, 4, 1)


def stage_weight(k, name):
    if name.startswith("max"):
        return 1
    return WEIGHTS_OF[min(max(k, 0), PHASES - 1)].get(name, 4)


def build(nc, x, adj, w0, a0s, a0d, beta0, wo0, w1, a1, w2, b2, gamma2, beta2, w3, b3, out):
    B, N, D = x.shape
    NT = N // P
    assert D == P and N == 2 * HALF and B % LANES == 0
    PAIRS = B // LANES
    tile0, group0, group_of = phase_plan(NT)
    slot_of, tile_before = ring_slots(tile0, len(group_of))
    QSCALE = float(HD) ** -0.5

    x_index = {}
    for span in ([-1], range(PHASES), [PHASES]):
        index = 0
        for k in span:
            for name in filter(uses_psX, side_uses(k)):
                x_index[k, name] = index
                index += 1

    def before(k, per_layer):
        return sum(per_layer[j // LANES] for j in range(k))

    def filled0(k):
        return before(k, (8 * NT, 0, 4 * NT, 4 * NT))

    def finished0(k):
        return before(k, (8 * NT, NT, 4 * NT, 0))

    def evac0(k):
        return before(k, (2, 2, 2 * NT, 4))

    def rho0(k):
        return before(k, (8, 1, 0, 0))

    def accumulated0(k):
        return before(k, (0, 0, 0, 2 * (NT - 1)))

    def residuals0(k):
        return {0: 0, 5: 1, 6: 3, 7: 5, PHASES: 0}[k]

    def chunks0(k):
        return before(k, (0, 0, 2 * NT, 0))

    def added0(k):
        return before(k, (0, 0, 2 * NT - 2, 0))

    def rho_at(k, h):
        return {2: 4, 3: 0}[k] if k >= LANES else (h + 2 * k) % RHOS

    ctx = ExitStack()
    with ctx:
        def sb(name, shape, dt=F32):
            return ctx.enter_context(nc.sbuf_tensor(name, shape, dt))

        def ps(name, shape):
            return ctx.enter_context(nc.psum_tensor(name, shape, F32))

        all_sems = []

        def sem(name, looped=True):
            s = ctx.enter_context(nc.semaphore(name))
            if looped:
                all_sems.append(s)
            return s

        edge = sb("edge", [P, NT, N])
        absent = sb("absent", [P, NT, N], BF16)
        ring = sb("ring", [P, RING, N])
        rho = sb("rho", [P, 4, N])
        xn = [sb(f"xn{s}", [P, NT, P]) for s in range(LANES)]
        xT = [sb(f"xT{s}", [P, N]) for s in range(LANES)]
        U = [sb(f"U{s}", [P, 2, N]) for s in range(LANES)]
        qs = [sb(f"qs{s}", [P, 4, N], F16) for s in range(LANES)]
        ks = [sb(f"ks{s}", [P, 4, N], F16) for s in range(LANES)]
        vals = [sb(f"vals{s}", [P, NT, P]) for s in range(LANES)]
        tmp = sb("tmp", [P, NT, P])
        rexp = sb("rexp", [P, NT, P])
        hilo = sb("hilo", [P, 2, 2, N], F16)
        identf = sb("identf", [P, P])
        identb = sb("identb", [P, P], BF16)
        ones = sb("ones", [P, P])
        selD = sb("selD", [P, 1])
        mhalf = sb("mhalf", [P, NT])
        wcat = [sb(f"wcat{l}", [P, P + HEADS[l]]) for l in range(2)]
        wsd = [sb(f"wsd{l}", [P, 2 * HEADS[l]]) for l in range(2)]
        woutp = sb("woutp", [P, 2, P])
        wt = {(l, n): sb(f"w{n}T{l}", [P, P]) for l in (2, 3) for n in "qkvo"}
        bcol = {(l, n): sb(f"b{n}{l}", [P, 1]) for l in (2, 3) for n in "qk"}
        bvB = {l: sb(f"bv{l}", [P, P]) for l in (2, 3)}
        boB = {l: sb(f"bo{l}", [P, P]) for l in (2, 3)}
        gammaB = sb("gammaB", [P, P])
        betaB = sb("betaB", [P, P])
        mx = sb("mx", [16, 1])
        diag = sb("diag", [16, 16])
        tops = sb("tops", [P, 16])
        tau = sb("tau", [P, 8])
        rbias = [sb(f"rbias{s}", [P, 8]) for s in range(LANES)]
        kap = [sb(f"kap{s}", [P, 8]) for s in range(LANES)]
        nkap = [sb(f"nkap{s}", [P, 8]) for s in range(LANES)]
        wj = [sb(f"wj{s}", [P, NT, 8]) for s in range(LANES)]
        dm = sb("dm", [P, 4, 8])
        gj = sb("gj", [P, 4, 8])
        gcol = [sb(f"gcol{s}", [P, NT, 32]) for s in range(LANES)]
        rn = sb("rn", [P, 64])
        stats = sb("stats", [P, NT, 6])
        mv = sb("mv", [P, NT, 2])
        veps = sb("veps", [P, NT])
        rstd = sb("rstd", [P, NT])
        mpart = sb("mpart", [P, 32, 2])
        mcol = sb("mcol", [P, 32])
        mrow = sb("mrow", [32, P], F16)
        betac = sb("betac", [P, 4])
        psS = ps("psS", [P, 2, N])
        psU = ps("psU", [P, 2, HALF])
        psX = ps("psX", [P, N])

        vpad = [qs[s][:, :, :].bitcast(F32).rearrange("p a (b h f) -> p (a b) h f", h=8, f=32)
                for s in range(LANES)]

        ring_tile = [ring[:, i, :] for i in range(RING)]
        for s in range(LANES):
            ring_tile += [ks[s][:, 2 * i:2 * i + 2, :].rearrange("p a n -> p (a n)").bitcast(F32) for i in range(2)]
        rho_buf = [rho[:, i, :] for i in range(4)]
        rho_buf += [hilo[:, i, :, :].rearrange("p a n -> p (a n)").bitcast(F32) for i in range(2)]

        chunk = rho[:, 1, :].rearrange("p (b n) -> p b n", b=2)
        rden = rho[:, 2, :].rearrange("p (b n) -> p b n", b=2)
        den_log = rho[:, 3, :].rearrange("p (b n) -> p b n", b=2)

        tile_sum = [[rho[:, 2 * half + p, :] for p in range(2)] for half in range(2)]

        s_x_in = [sem(f"x_in{s}") for s in range(LANES)]
        s_zeroed = sem("vpad_zeroed")
        s_ones_row = sem("ones_row_ready")
        s_xw = sem("psX_written")
        s_xr = sem("psX_read")
        s_diag = sem("diag_ready")
        s_tau = sem("tau_ready")
        s_kap = sem("kappa_ready")
        s_nkap = sem("minus_kappa_ready")
        s_dm = sem("dst_minus_top_ready")
        s_wj = sem("w_and_g_ready")
        s_vals = sem("values_ready")
        s_res = sem("residual_plus_bias_ready")
        s_norm = sem("sums_normalised")
        s_veps = sem("variance_ready")
        s_rstd = sem("rstd_ready")
        s_centred = sem("mean_subtracted")
        s_xn = sem("xn_ready")
        s_hi = sem("qk_full_and_hi_ready")
        s_lo = sem("qk_lo_ready")
        s_stack = {(l, s): sem(f"stacked{l}{s}") for l in (2, 3) for s in range(LANES)}
        s_mcol = sem("max_columns_ready")
        s_mrow = sem("max_rows_ready")
        s_rho_ps = sem("rho_in_psum")
        s_rho = sem("rho_ready")
        s_scores = sem("scores_ready")
        s_filled = sem("tile_filled")
        s_finished = sem("tile_finished")
        s_used = sem("tile_group_used")
        s_evac = sem("sums_out_of_psum")
        s_chain = sem("vector_chain")
        s_den = sem("denominators_ready")
        s_rden = sem("chunk_reciprocals_ready")
        s_scaled = sem("chunk_normalised")
        s_added = sem("chunk_added")
        s_tsum = (sem("tile_added_heads_01"), sem("tile_added_heads_23"))
        s_dsum = sem("row_sums_ready")
        s_out = sem("stored")
        s_done = {e: sem(f"{e}_at_end") for e in ("pe", "act", "dve", "pool")}
        s_go = sem("pair_done", looped=False)
        s_load = sem("weights_loaded", looped=False)
        s_adj = sem("adj_loaded", looped=False)
        s_adjf = sem("adj_as_float", looped=False)
        s_adjT = sem("adj_transposed", looped=False)
        s_adjr = sem("adj_T_out", looped=False)
        s_ln = sem("log_ready", looped=False)
        s_pw = sem("power_ready", looped=False)
        s_id = sem("identity_ready", looped=False)
        s_ones = sem("ones_ready", looped=False)
        s_wT = sem("weight_transposed", looped=False)
        s_wTr = sem("weight_T_out", looped=False)
        s_wpad = sem("wout_padded", looped=False)
        s_b = sem("beta_ready", looped=False)
        s_vset = sem("vector_setup_chain", looped=False)
        s_aset = sem("scalar_setup_chain", looped=False)
        s_setup = sem("setup_done", looped=False)

        adj_i = ring[:, 0:NT, :].bitcast(I32)
        adj_f = ring[:, 0:NT, :]
        stage = [t[:, :, :].bitcast(F32).rearrange("p a n -> p (a n)") for t in (*qs, *ks)]
        adj_eps = [stage[t // 2][:, (t % 2) * N:(t % 2 + 1) * N] for t in range(NT)]
        raw = {("o", 0): rho[:, 0, 0:P]}
        for i, key in enumerate([(n, l) for l in (2, 3) for n in "qkvo"]):
            raw[key] = rho[:, 1, i * P:(i + 1) * P]
        wpad = rho[:, 0, 256:512].rearrange("p (g q r) -> p g q r", g=2, q=4)
        a_row = {0: rho[:, 2, 0:256], 1: rho[:, 2, 256:512]}
        prod = rho[:, 3, 0:P]
        WEIGHTS = [("q", 2), ("k", 2), ("v", 2), ("o", 2), ("q", 3), ("k", 3), ("v", 3), ("o", 3)]

        def lane_of(k):
            return k % LANES

        def due(t, tiles, k):
            weights = [stage_weight(k, name) for name in side_uses(k)]
            return sum(sum(weights[:i]) * tiles < t * sum(weights) for i in range(len(weights)))

        def due_reader(t, tiles, k, engine):
            group, lag = (4, 1, 2, 2)[k // LANES], LAG[engine][k]
            return due(max(0, t // group * group - lag), tiles, k)

        def chunks_before_norm(k):
            uses, tiles = side_uses(k), 4 * NT
            n = next(n for n in range(tiles) if due_reader(n + 1, tiles, k, "dve") > uses.index("out"))
            return (n - 1) // 2 if n >= 3 else 0

        def units_before_norm(k):
            uses, tiles = side_uses(k), 4 * NT
            return next(n + 1 for n in range(tiles) if due_reader(n + 1, tiles, k, "dve") > uses.index("out")) // 2

        def norm_by_gpsimd(k):
            return 0 <= k < LANES

        def adds_pair(k, n):
            return k == 3 * LANES and n >= PAIR_FROM

        def add_tile(engine, vector, p, k, n):
            half, jt = n // NT, n % NT
            if jt == 0:
                return
            done = accumulated0(k) + (NT - 1) * half + jt - 1
            engine.wait_ge(s_filled, filled0(k) + 2 * n + p + 1)
            if done:
                engine.wait_ge(s_tsum[p], done)
            if jt == 1 and k == PHASES - 1:
                engine.wait_ge(s_dsum, half + 1)
            t = tile0[k] + 2 * n + p
            total = tile_sum[half][p]
            first = ring_tile[slot_of[t - 2]] if jt == 1 else total
            vector.tensor_tensor(total, first, ring_tile[slot_of[t]], ALU.add).then_inc(s_tsum[p], 1)

        block = ctx.enter_context(nc.Block())

        @block.sync
        def _(sp):
            loads = [
                (wcat[0][:, 0:P].rearrange("p (h f) -> p h f", h=8), w0.rearrange("h d f -> d h f")),
                (wcat[1][:, 0:P], w1),
                (a_row[0][:, 0:P], a0s.rearrange("(o h) f -> o (h f)", o=1).broadcast_to([P, P])),
                (a_row[0][:, P:2 * P], a0d.rearrange("(o h) f -> o (h f)", o=1).broadcast_to([P, P])),
                (a_row[1], a1.rearrange("n o -> o n").broadcast_to([P, 2 * P])),
                (raw["o", 0], wo0),
                (betac[:, 0:1], beta0.broadcast_to([P, 1])),
                (gammaB[:, :], gamma2.rearrange("(o n) -> o n", o=1).broadcast_to([P, P])),
                (betaB[:, :], beta2.rearrange("(o n) -> o n", o=1).broadcast_to([P, P])),
            ]
            for l, w, b in ((2, w2, b2), (3, w3, b3)):
                loads += [(raw[n, l], w[n]) for n in "qkvo"]
                loads += [(bcol[l, n][:, :], b[n].rearrange("(p o) -> p o", o=1)) for n in "qk"]
                loads += [(bvB[l][:, :], b["v"].rearrange("(o n) -> o n", o=1).broadcast_to([P, P])),
                          (boB[l][:, :], b["o"].rearrange("(o n) -> o n", o=1).broadcast_to([P, P]))]
            for t in range(NT):
                sp.dma_start(adj_i[:, t, :], adj[t * P:(t + 1) * P, :]).then_inc(s_adj, 16)
            for dst, src in loads:
                sp.dma_start(dst, src).then_inc(s_load, 16)
            assert len(loads) == N_LOADS
            def nodes(t, b):
                return t[b, :, :].rearrange("(t p) d -> p t d", p=P)

            def all_counts_to_zero():
                for e in s_done.values():
                    sp.wait_ge(e, 1)
                for q in all_sems:
                    sp.sem_clear(q)
                sp.sem_inc(s_go, 1)

            for s in range(LANES):
                sp.dma_start(xn[s][:, :, :], nodes(x, s * PAIRS)).then_inc(s_x_in[s], 16)
            sp.wait_ge(s_x_in[1], 16)
            all_counts_to_zero()

            with sp.Fori(0, PAIRS) as pair:
                sp.wait_ge(s_xn, 1)
                sp.dma_start(nodes(out, PAIRS - 1 + pair), xn[1][:, :, :]).then_inc(s_out, 16)
                sp.wait_ge(s_out, 16)
                sp.dma_start(xn[1][:, :, :], nodes(x, PAIRS + pair)).then_inc(s_x_in[1], 16)
                for k in range(2 * LANES, PHASES):
                    l, s = k // LANES, lane_of(k)
                    if l == 3:
                        sp.wait_ge(s_used, group0[k - LANES + 1])
                    for m, (dst, parts) in enumerate(((qs[s], (0, 0, 1)), (ks[s], (0, 1, 0)))):
                        sp.wait_ge(s_hi, 2 * (k - 4) + m + 1)
                        sp.wait_ge(s_lo, 2 * (k - 4) + m + 1)
                        for h in range(4):
                            for r, part in enumerate(parts):
                                sp.dma_start(dst[r * HD:(r + 1) * HD, h, :],
                                             hilo[h * HD:(h + 1) * HD, m, part, :]).then_inc(s_stack[l, s], 16)
                    if l == 3:
                        sp.wait_ge(s_mrow, k - 6 + 1)
                        sp.dma_start(qs[s][SPLIT_ROWS:SPLIT_ROWS + 1, :, :].rearrange("p h (t i) -> p (h t) i", i=P),
                                     mrow[:, :]).then_inc(s_stack[l, s], 16)
                sp.wait_ge(s_xn, PHASES)
                sp.dma_start(nodes(out, pair), xn[0][:, :, :]).then_inc(s_out, 16)
                sp.wait_ge(s_out, 32)
                sp.dma_start(xn[0][:, :, :], nodes(x, pair + 1)).then_inc(s_x_in[0], 16)
                sp.wait_ge(s_x_in[0], 16)
                all_counts_to_zero()
            sp.wait_ge(s_xn, 1)
            sp.dma_start(nodes(out, B - 1), xn[1][:, :, :]).then_inc(s_out, 16)
            sp.wait_ge(s_out, 16)

        @block.gpsimd
        def _(pool):
            def zero_vpad(s, count):
                nc.gpsimd.memset(vpad[s], 0.0).then_inc(s_zeroed, 1)
                pool.wait_ge(s_zeroed, count)

            norms = 0

            def rstds(count):
                nonlocal norms
                for _ in range(count):
                    norms += 1
                    pool.wait_ge(s_veps, norms)
                    nc.gpsimd.tensor_tensor(rstd[:, :], veps[:, :], mhalf[:, :], ALU.pow).then_inc(s_rstd, 1)

            def residuals(k):
                j = epilogue_of(k)
                l, s = j // LANES, lane_of(j)
                if 1 <= k < PHASES:
                    pool.wait_ge(s_lo, 2 * (k - 3))
                for i, (dst, bias) in enumerate(((tmp, boB[l]), (rexp, betaB))[:2 if l == 2 else 1]):
                    nc.gpsimd.tensor_tensor(dst[:, :, :], xn[s][:, :, :],
                                            bias[:, :].unsqueeze(1).broadcast_to([P, NT, P]), ALU.add).then_inc(s_res, 1)

            nc.gpsimd.memset(ones[:, :], 1.0).then_inc(s_ones, 1)
            nc.gpsimd.memset(mhalf[:, :], -0.5).then_inc(s_ones, 1)
            nc.gpsimd.memset(identf[:, :], 0.0).then_inc(s_id, 1)
            pool.wait_ge(s_id, 1)
            nc.gpsimd.affine_select(out=identf[:, :], in_=identf[:, :], compare_op=ALU.not_equal, fill=1.0,
                                    base=0, pattern=[[-1, P]], channel_multiplier=1).then_inc(s_id, 1)
            pool.wait_ge(s_id, 2)
            nc.gpsimd.tensor_copy(identb[:, :], identf[:, :]).then_inc(s_id, 1)
            nc.gpsimd.memset(U[1][:, :, :], 1.0).then_inc(s_id, 1)
            pool.wait_ge(s_id, 4)
            pool.wait_ge(s_setup, 1)
            zero_vpad(0, 1)
            pool.sem_inc(s_done["pool"], 1)
            pool.wait_ge(s_go, 1)

            with pool.Fori(0, PAIRS) as pair:
                residuals(0)
                zero_vpad(1, 1)
                norms = 0
                for k in range(PHASES):
                    l, s = k // LANES, lane_of(k)
                    if k == LANES:
                        pool.wait_ge(s_used, group0[LANES])
                        for i in range(LANES):
                            nc.gpsimd.memset(ks[i][SPLIT_ROWS:SPLIT_ROWS + 1, :, :], 1.0).then_inc(s_ones_row, 1)
                            pool.wait_ge(s_ones_row, i + 1)
                    norms_in_side = 2 if epilogue_of(k) // LANES == 2 else 1
                    if k >= 1 and epilogue_of(k) >= 2 * LANES:
                        residuals(k)
                    if k == PHASES - 1:
                        pool.wait_ge(s_used, group0[k])
                        zero_vpad(0, 2)
                    if l == 2:
                        n_added = added0(k)
                        for n in range(2 * NT):
                            half = n // NT
                            if n == chunks_before_norm(k):
                                rstds(norms_in_side)
                            if n % NT:
                                pool.wait_ge(s_scaled, chunks0(k) + n + 1)
                                if n_added:
                                    pool.wait_ge(s_added, n_added)
                                part = U[s][:, 0, half * HALF:(half + 1) * HALF]
                                nc.gpsimd.tensor_tensor(part, part, chunk[:, n % 2, :], ALU.add).then_inc(s_added, 1)
                                n_added += 1
                    elif l == 3:
                        if k == 3 * LANES:
                            pool.wait_ge(s_scaled, chunks0(k))
                            pool.wait_ge(s_added, added0(k))
                        for n in range(2 * NT):
                            if n == units_before_norm(k):
                                rstds(norms_in_side)
                            for p in range(1 + adds_pair(k, n)):
                                add_tile(pool, nc.gpsimd, p, k, n)
                        if units_before_norm(k) >= 2 * NT:
                            rstds(norms_in_side)
                    elif norm_by_gpsimd(k):
                        rstds(1)
                        j = lane_of(epilogue_of(k))
                        pool.wait_ge(s_rstd, norms)
                        nc.gpsimd.tensor_tensor(tmp[:, :, :], tmp[:, :, :], mv[:, :, 0:1].broadcast_to([P, NT, P]),
                                                ALU.subtract).then_inc(s_centred, 1)
                        pool.wait_ge(s_centred, k + 1)
                        nc.gpsimd.tensor_tensor(xn[j][:, :, :], tmp[:, :, :],
                                                rstd[:, :].unsqueeze(2).broadcast_to([P, NT, P]), ALU.mult)\
                            .then_inc(s_xn, 1)
                    else:
                        rstds(norms_in_side)
                pool.sem_inc(s_done["pool"], 1)
                pool.wait_ge(s_go, pair + 2)
            norms = 0
            residuals(PHASES)
            rstds(1)

        @block.scalar
        def _(act):
            act.wait_ge(s_load, 16 * N_LOADS)
            act.wait_ge(s_b, 1)
            act.wait_ge(s_ones, 2)
            nc.scalar.activation(betac[:, 2:3], betac[:, 1:2], ACT.Exp).then_inc(s_aset, 1)
            act.wait_ge(s_aset, 1)
            nc.scalar.activation(betac[:, 3:4], betac[:, 2:3], ACT.Ln, bias=ones[:, 0:1]).then_inc(s_aset, 1)
            for t in range(NT):
                act.wait_ge(s_adjr, t + 1)
                nc.scalar.activation(edge[:, t, :], adj_eps[t], ACT.Ln).then_inc(s_ln, 1)
            act.wait_ge(s_b, 2)
            act.wait_ge(s_ln, NT)
            for t in range(NT):
                nc.scalar.activation(edge[:, t, :], edge[:, t, :], ACT.Exp, scale=betac[:, 1:2]).then_inc(s_pw, 1)
            act.wait_ge(s_setup, 1)

            def gat_rho(k, h):
                l, s = k // LANES, lane_of(k)
                act.wait_ge(s_rho_ps, rho0(k) + h + 1)
                if h >= RHOS:
                    act.wait_ge(s_filled, filled0(k) + 4 * NT)
                elif k >= 1:
                    act.wait_ge(s_filled, filled0(k) - (4 * NT if k <= LANES and h < 2 else 0))
                    if k - 1 >= LANES:
                        act.wait_ge(s_finished, finished0(k))
                nc.scalar.activation(rho_buf[rho_at(k, h)], psS[:, (h + l) % 2, :], ACT.Exp,
                                     bias=rbias[s][:, h:h + 1], scale=1.0 - SLOPE[l]).then_inc(s_rho, 1)

            def side(k):
                for name in side_uses(k):
                    m = x_index.get((k, name))
                    s = lane_of(prologue_of(k))
                    l = prologue_of(k) // LANES
                    n_gat = gat_before(prologue_of(k)) if k >= 0 else 0
                    if name == "xT":
                        act.wait_ge(s_xw, m + 1)
                        nc.scalar.activation(xT[s][:, :], psX[:, :], ACT.Copy).then_inc(s_xr, 1)
                    elif name == "top_bc":
                        act.wait_ge(s_tau, n_gat + 1)
                        nc.scalar.activation(kap[s][:, 0:HEADS[l]], tau[:, 0:HEADS[l]], ACT.Exp, scale=-1.0)\
                            .then_inc(s_kap, 1)
                    elif name in ("values0", "values1"):
                        half = int(name[-1])
                        H = HEADS[l]
                        act.wait_ge(s_dm, 2 * n_gat + half + 1)
                        nc.scalar.activation(wj[s][:, 4 * half:4 * half + 4, 0:H], dm[:, :, 0:H], ACT.Exp,
                                             scale=1.0 - SLOPE[l])
                        nc.scalar.activation(gj[:, :, 0:H], dm[:, :, 0:H], ACT.Exp, scale=SLOPE[l]).then_inc(s_wj, 1)
                    elif name in ("q", "k"):
                        q = name == "q"
                        act.wait_ge(s_xw, m + 1)
                        i = 2 * (k + 1 - 4) + (not q)
                        if i >= 1:
                            act.wait_ge(s_lo, i)
                        if i >= 2:
                            j = i // 2 - 1
                            act.wait_ge(s_stack[2 + j // LANES, j % LANES], 24 * 16)
                        nc.scalar.activation(tmp[:, :, :].rearrange("p a b -> p (a b)"), psX[:, :], ACT.Identity,
                                             bias=bcol[l, name][:, :], scale=QSCALE if q else 1.0).then_inc(s_xr, 1)
                        act.wait_ge(s_xr, m + 1)
                        nc.scalar.activation(hilo[:, 1 - q, 0, :], tmp[:, :, :].rearrange("p a b -> p (a b)"),
                                             ACT.Copy).then_inc(s_hi, 1)
                    elif name == "max_rows":
                        act.wait_ge(s_xw, m + 1)
                        nc.scalar.activation(mrow[:, :], psX[0:32, 0:P], ACT.Copy, scale=-1.0).then_inc(s_mrow, 1)
                        act.wait_ge(s_mrow, k + 1 - 6 + 1)
                        act.sem_inc(s_xr, 1)
                    yield

            def free_slot(t):
                if tile_before[t] is not None:
                    b = tile_before[t]
                    act.wait_ge(s_used, group_of[b] + 1)
                    if b >= tile0[3 * LANES]:
                        k, n = 3 * LANES + (b - tile0[3 * LANES]) // (4 * NT), (b - tile0[3 * LANES]) % (4 * NT)
                        half, jt = n // (2 * NT), n // 2 % NT
                        act.wait_ge(s_tsum[n % 2], accumulated0(k) + (NT - 1) * half + max(jt, 1))

            def gat_fill(k, n):
                s, t = lane_of(k), tile0[k] + n
                h, jt = n // (4 * NT) * 4 + n % 4, n % (4 * NT) // 4
                free_slot(t)
                act.wait_ge(s_rho, rho0(k) + h + 1)
                nc.scalar.activation(ring_tile[slot_of[t]], rho_buf[rho_at(k, h)], ACT.Relu,
                                     bias=nkap[s][:, h:h + 1], scale=wj[s][:, jt, h:h + 1]).then_inc(s_filled, 1)

            def gat_start(k):
                if k >= 1:
                    act.wait_ge(s_nkap, gat_before(k) + 1)
                    act.wait_ge(s_wj, 2 * (gat_before(k) + 1))
                if k < LANES:
                    if k == 1:
                        gat_rho(k, 2)
                        gat_rho(k, 3)
                    for n in range(4):
                        if k == 0:
                            gat_rho(k, n)
                        gat_fill(k, n)
                elif k > LANES:
                    gat_rho(k, 0)

            def gat_sums_out(k, g):
                act.wait_ge(s_used, group0[k] + NT * (g + 1))
                nc.scalar.activation(U[lane_of(k)][:, g, :], psU[:, :, :].rearrange("p a b -> p (a b)"),
                                     ACT.Copy).then_inc(s_evac, 1)

            for _ in side(-1):
                pass
            act.sem_inc(s_done["act"], 1)
            act.wait_ge(s_go, 1)

            with act.Fori(0, PAIRS) as pair:
                for k in range(PHASES):
                    l, s = k // LANES, lane_of(k)
                    stages = side(k)
                    done = 0
                    tiles = {0: 8 * NT, 1: NT, 2: 4 * NT, 3: 4 * NT}[l]

                    def advance(t):
                        nonlocal done
                        while done < due_reader(t, tiles, k, "act"):
                            next(stages)
                            done += 1

                    if l == 0:
                        if k == 0:
                            gat_start(k)
                        for n in range(4, 8 * NT):
                            if n in (8, 12):
                                gat_rho(k, 4 + (n == 12))
                            if n == 4 * NT:
                                gat_rho(k, 6)
                                gat_rho(k, 7)
                            if n == 7 * NT:
                                act.wait_ge(s_tau, k + 1)
                                for h in range(2 if k + 1 < LANES else 1):
                                    gat_rho(k + 1, h)
                            gat_fill(k, n)
                            if n == 4 * NT + 3:
                                gat_sums_out(k, 0)
                            advance(n + 1)
                        for _ in stages:
                            pass
                        gat_start(k + 1)
                        gat_sums_out(k, 1)
                    elif l == 1:
                        if k > LANES:
                            gat_start(k)
                        for n in range(NT):
                            advance(n + 1)
                        act.wait_ge(s_used, group0[k + 1])
                        nc.scalar.activation(U[s][:, 0, :], psU[:, :, :].rearrange("p a b -> p (a b)"),
                                             ACT.Copy).then_inc(s_evac, 1)
                        nc.scalar.activation(U[s][:, 1, :], psS[:, 0, :], ACT.Copy).then_inc(s_evac, 1)
                    else:
                        def reciprocals(n):
                            i = chunks0(k) + n
                            act.wait_ge(s_den, i + 1)
                            if i >= 2:
                                act.wait_ge(s_rden, i - 1)
                            nc.scalar.activation(den_log[:, n % 2, :], psU[:, 1, :], ACT.Ln).then_inc(s_evac, 1)
                            act.wait_ge(s_evac, evac0(k) + n + 1)
                            if i >= 2:
                                act.wait_ge(s_scaled, i - 1)
                            nc.scalar.activation(rden[:, n % 2, :], den_log[:, n % 2, :], ACT.Exp, scale=-1.0).then_inc(s_rden, 1)

                        def evacuate(half, bank):
                            if bank == 0:
                                act.wait_ge(s_used, group0[k] + NT * (half + 1))
                            else:
                                act.wait_ge(s_dsum, 2 * (k - 3 * LANES) + half + 1)
                            nc.scalar.activation(U[s][:, bank, half * HALF:(half + 1) * HALF], psU[:, bank, :],
                                                 ACT.Copy).then_inc(s_evac, 1)

                        for n in range(2 * NT):
                            for p in range(2):
                                t = tile0[k] + 2 * n + p
                                act.wait_ge(s_scores, 4 * NT * (k - 4) + 2 * n + p + 1)
                                free_slot(t)
                                nc.scalar.activation(ring_tile[slot_of[t]], psS[:, p, :], ACT.Exp).then_inc(s_filled, 1)
                                if l == 2 and n >= 1 and p == 1:
                                    reciprocals(n - 1)
                                if l == 3 and n in (NT, NT + 1) and p == 1:
                                    evacuate(0, n - NT)
                                advance(2 * n + p + 1)
                        if l == 2:
                            reciprocals(2 * NT - 1)
                        else:
                            evacuate(1, 0)
                            evacuate(1, 1)
                    for _ in stages:
                        pass
                act.wait_ge(s_evac, evac0(PHASES))
                act.sem_inc(s_done["act"], 1)
                act.wait_ge(s_go, pair + 2)

        @block.vector
        def _(dve):
            link_n = [0]
            chain = [s_vset]

            def link(ins):
                link_n[0] += 1
                ins.then_inc(chain[0], 1)
                dve.wait_ge(chain[0], link_n[0])

            dve.wait_ge(s_adj, 16 * NT)
            for it in range(NT):
                nc.vector.tensor_copy(adj_f[:, it, :], adj_i[:, it, :]).then_inc(s_adjf, 1)
            dve.wait_ge(s_load, 16 * N_LOADS)
            link(nc.vector.tensor_scalar(betac[:, 1:2], betac[:, 0:1], -1.0, None, ALU.mult))
            nc.vector.tensor_tensor(betac[:, 1:2], betac[:, 0:1], betac[:, 1:2], ALU.min).then_inc(s_b, 1)
            dve.wait_ge(s_aset, 2)
            nc.vector.scalar_tensor_tensor(betac[:, 1:2], betac[:, 0:1], 0.0, betac[:, 3:4], ALU.max, ALU.add)\
                .then_inc(s_b, 1)
            for l in range(2):
                H = HEADS[l]
                for side_ in range(2):
                    link(nc.vector.tensor_tensor(prod, wcat[l][:, 0:P], a_row[l][:, side_ * P:(side_ + 1) * P], ALU.mult))
                    link(nc.vector.tensor_reduce(wsd[l][:, side_ * H:(side_ + 1) * H],
                                                 prod.rearrange("p (h f) -> p h f", h=H), AX.X, ALU.add))
                link(nc.vector.tensor_copy(wcat[l][:, P:P + H], wsd[l][:, H:2 * H]))
            link(nc.vector.memset(rho[:, 0, 256:512], 0.0))
            nc.vector.tensor_copy(wpad[:, :, :, 0:16],
                                  raw["o", 0].rearrange("p (g q r) -> p g q r", g=2, q=4)).then_inc(s_wpad, 1)
            dve.wait_ge(s_id, 3)
            link(nc.vector.tensor_reduce(selD[:, :], identf[:, 0:P:32], AX.X, ALU.add))
            for jt in range(NT):
                dve.wait_ge(s_adjT, jt + 1)
                nc.vector.tensor_scalar(absent[:, jt, :], psS[:, jt % 2, :], 0.0, ABSENT, ALU.is_equal, ALU.mult)
                nc.vector.tensor_scalar(adj_eps[jt], psS[:, jt % 2, :], 0.0, EPS_LOG, ALU.max, ALU.add)\
                    .then_inc(s_adjr, 1)
            for i, (n, l) in enumerate(WEIGHTS):
                dve.wait_ge(s_wT, i + 1)
                nc.vector.tensor_copy(wt[l, n][:, :], psX[:, (i % 2) * HALF:(i % 2) * HALF + P]).then_inc(s_wTr, 1)
            for g in range(2):
                i = len(WEIGHTS) + g
                dve.wait_ge(s_wT, i + 1)
                nc.vector.tensor_copy(woutp[:, g, :], psX[:, (i % 2) * HALF:(i % 2) * HALF + P]).then_inc(s_wTr, 1)
            for l in (2, 3):
                link(nc.vector.tensor_scalar(bcol[l, "q"][:, :], bcol[l, "q"][:, :], QSCALE, None, ALU.mult))
            for t in range(NT):
                dve.wait_ge(s_pw, t + 1)
                link(nc.vector.scalar_tensor_tensor(edge[:, t, :], adj_eps[t], EPS_LOG, edge[:, t, :],
                                                    ALU.is_gt, ALU.mult))
            nc.vector.memset(veps[:, :], 0.0).then_inc(s_setup, 1)
            chain[0] = s_chain

            def gat_prologue(k, name, m):
                l, s = prologue_of(k) // LANES, lane_of(prologue_of(k))
                n, H, lam = gat_before(prologue_of(k)) if k >= 0 else 0, HEADS[l], 1.0 - SLOPE[l]
                if name == "tops":
                    dve.wait_ge(s_xw, m + 1)
                    nc.vector.tensor_reduce(mx[0:2 * H, :], psX[0:2 * H, :], AX.X, ALU.max).then_inc(s_xr, 1)
                    dve.wait_ge(s_xr, m + 1)
                    nc.vector.tensor_scalar(diag[0:2 * H, 0:2 * H], identf[0:2 * H, 0:2 * H], mx[0:2 * H, :], None,
                                            ALU.mult).then_inc(s_diag, 1)
                elif name == "top_bc":
                    dve.wait_ge(s_xw, m + 1)
                    nc.vector.tensor_copy(tops[:, 0:2 * H], psX[:, 0:2 * H]).then_inc(s_xr, 1)
                    dve.wait_ge(s_xr, m + 1)
                    link(nc.vector.tensor_tensor(tau[:, 0:H], tops[:, 0:H], tops[:, H:2 * H], ALU.add))
                    link(nc.vector.tensor_scalar(tau[:, 0:H], tau[:, 0:H], lam, -TAU_START, ALU.mult, ALU.add))
                    link(nc.vector.tensor_scalar(tau[:, 0:H], tau[:, 0:H], 0.0, None, ALU.max))
                    nc.vector.scalar_tensor_tensor(rbias[s][:, 0:H], tops[:, H:2 * H], lam, tau[:, 0:H],
                                                   ALU.mult, ALU.subtract).then_inc(s_tau, 1)
                elif name == "kappa":
                    dve.wait_ge(s_kap, n + 1)
                    nc.vector.tensor_scalar(nkap[s][:, 0:H], kap[s][:, 0:H], -1.0, None, ALU.mult).then_inc(s_nkap, 1)
                elif name in ("values0", "values1"):
                    half = int(name[-1])
                    dve.wait_ge(s_xw, m + 1)
                    if 2 * n + half >= 1:
                        dve.wait_ge(s_wj, 2 * n + half)
                    v = psX[:, :].rearrange("p (t c) -> p t c", c=2 * P)
                    nc.vector.tensor_tensor(dm[:, :, 0:H], v[:, :, P:P + H],
                                            tops[:, H:2 * H].unsqueeze(1).broadcast_to([P, 4, H]), ALU.subtract)\
                        .then_inc(s_dm, 1)
                else:
                    half = int(name[-1])
                    jts = slice(4 * half, 4 * half + 4)
                    v = psX[:, :].rearrange("p (t c) -> p t c", c=2 * P)
                    dve.wait_ge(s_wj, 2 * n + half + 1)
                    if l == 0:
                        if half == 0:
                            dve.wait_ge(s_zeroed, 2 if k == PHASES - 1 else 1)
                        nc.vector.tensor_copy(vpad[s][:, jts, :, 16:17], gj[:, :, 0:H].unsqueeze(3)).then_inc(s_vals, 1)
                        nc.vector.tensor_tensor(vpad[s][:, jts, :, 0:16],
                                                v[:, :, 0:P].rearrange("p t (h f) -> p t h f", h=H),
                                                gj[:, :, 0:H].unsqueeze(3).broadcast_to([P, 4, H, 16]), ALU.mult)\
                            .then_inc(s_xr, 1)
                    else:
                        nc.vector.tensor_copy(gcol[s][:, jts, :], gj[:, :, 0:1].broadcast_to([P, 4, 32]))\
                            .then_inc(s_vals, 1)
                        nc.vector.tensor_tensor(vals[s][:, jts, :], v[:, :, 0:P],
                                                gj[:, :, 0:1].broadcast_to([P, 4, P]), ALU.mult).then_inc(s_xr, 1)

            norms = [0]

            def normalise(dst, src, gamma=None, residual=None, on_gpsimd=False):
                for t in range(NT):
                    ins = nc.vector.bn_stats(stats[:, t, :], src[:, t, :])
                link(ins)
                for t in range(NT):
                    ins = nc.vector.bn_aggr(mv[:, t, :], stats[:, t, :])
                link(ins)
                norms[0] += 1
                nc.vector.tensor_scalar(veps[:, :], mv[:, :, 1], EPS_LN, None, ALU.add).then_inc(s_veps, 1)
                if on_gpsimd:
                    return None
                nc.vector.tensor_tensor(src[:, :, :], src[:, :, :], mv[:, :, 0:1].broadcast_to([P, NT, P]), ALU.subtract)\
                    .then_inc(chain[0], 1)
                link_n[0] += 1
                if gamma is not None:
                    dve.wait_ge(chain[0], link_n[0])
                    nc.vector.tensor_tensor(src[:, :, :], src[:, :, :],
                                            gamma[:, :].unsqueeze(1).broadcast_to([P, NT, P]), ALU.mult)\
                        .then_inc(chain[0], 1)
                    link_n[0] += 1
                dve.wait_ge(chain[0], link_n[0])
                dve.wait_ge(s_rstd, norms[0])
                if residual is None:
                    return nc.vector.tensor_tensor(dst[:, :, :], src[:, :, :],
                                                   rstd[:, :].unsqueeze(2).broadcast_to([P, NT, P]), ALU.mult)
                for t in range(NT):
                    ins = nc.vector.scalar_tensor_tensor(dst[:, t, :], src[:, t, :], rstd[:, t:t + 1],
                                                         residual[:, t, :], ALU.mult, ALU.add)
                return ins

            def epilogue(k, name, m):
                l, s = epilogue_of(k) // LANES, lane_of(epilogue_of(k))
                ps3 = psX[:, :].rearrange("p (t d) -> p t d", d=P)
                if uses_psX(name):
                    dve.wait_ge(s_xw, m + 1)

                if name == "norm":
                    if 1 <= k < PHASES:
                        dve.wait_ge(s_evac, evac0(k))
                    blocks = N // 32
                    work = [rexp, tmp][:2 if l == 0 else 1]
                    flat = [w[:, :, :].rearrange("p a b -> p (a b)") for w in work]
                    if 1 <= k <= LANES:
                        dve.wait_ge(s_xn, k)
                    for g, w in enumerate(flat):
                        ins = nc.vector.transpose(w, U[s][:, g if l == 0 else 1, :])
                    link(ins)
                    for g, w in enumerate(flat):
                        sums, r = w.rearrange("p (b c) -> p b c", c=32)[:, :, 16], rn[:, g * blocks:(g + 1) * blocks]
                        if l == 3:
                            link(nc.vector.tensor_scalar(r, sums, 1e-37, None, ALU.max))
                            sums = r
                        ins = nc.vector.reciprocal(r, sums)
                    link(ins)
                    for g, w in enumerate(flat):
                        ins = nc.vector.transpose(w, rn[:, g * blocks:(g + 1) * blocks].unsqueeze(2)
                                                  .broadcast_to([P, blocks, 32]))
                    link(ins)
                    for g, w in enumerate(flat):
                        ins = nc.vector.tensor_tensor(U[s][:, g, :], U[s][:, g, :], w, ALU.mult)
                    ins.then_inc(s_norm, 1)
                elif name == "den":
                    nc.vector.reciprocal(rn[:, 0:NT], psX[:, 0:NT]).then_inc(s_xr, 1)
                    dve.wait_ge(s_xr, m + 1)
                elif name == "out":
                    if l == 1:
                        nc.vector.scalar_tensor_tensor(tmp[:, :, :], ps3, 0.0,
                                                       rn[:, 0:NT].unsqueeze(2).broadcast_to([P, NT, P]),
                                                       ALU.max, ALU.mult).then_inc(s_xr, 1)
                        dve.wait_ge(s_xr, m + 1)
                        link(nc.vector.tensor_tensor(tmp[:, :, :], tmp[:, :, :], xn[s][:, :, :], ALU.add))
                    else:
                        residual = xn[s]
                        if l >= 2:
                            residual = tmp
                            dve.wait_ge(s_res, residuals0(k) + (2 if l == 2 else 1))
                        nc.vector.tensor_tensor(tmp[:, :, :], ps3, residual[:, :, :], ALU.add).then_inc(s_xr, 1)
                        dve.wait_ge(s_xr, m + 1)
                    if l == 2:
                        link(normalise(tmp, tmp, gammaB, rexp))
                    if norm_by_gpsimd(k):
                        normalise(xn[s], tmp, on_gpsimd=True)
                    else:
                        if k == LANES:
                            dve.wait_ge(s_xn, k)
                        normalise(xn[s], tmp).then_inc(s_xn, 1)

            def side(k):
                in_epilogue = k >= 0
                for name in side_uses(k):
                    m = x_index.get((k, name))
                    if name == "xT":
                        in_epilogue = False
                    l, s = prologue_of(k) // LANES, lane_of(prologue_of(k))
                    if in_epilogue:
                        epilogue(k, name, m)
                    elif name in ("tops", "top_bc", "kappa", "values0", "g0", "values1", "g1"):
                        gat_prologue(k, name, m)
                    elif name in ("q", "k"):
                        q = name == "q"
                        i = 2 * (k + 1 - 4) + (not q)
                        dve.wait_ge(s_hi, i + 1)
                        if i >= 2:
                            j = i // 2 - 1
                            dve.wait_ge(s_stack[2 + j // LANES, j % LANES], 24 * 16)
                        nc.vector.tensor_tensor(hilo[:, 1 - q, 1, :], tmp[:, :, :].rearrange("p a b -> p (a b)"),
                                                hilo[:, 1 - q, 0, :], ALU.subtract).then_inc(s_lo, 1)
                    elif name == "v":
                        dve.wait_ge(s_xw, m + 1)
                        nc.vector.tensor_tensor(vals[s][:, :, :], psX[:, :].rearrange("p (t d) -> p t d", d=P),
                                                bvB[l][:, :].unsqueeze(1).broadcast_to([P, NT, P]), ALU.add)\
                            .then_inc(s_xr, 1)
                    elif name.startswith("max") and name != "max_rows":
                        i = int(name[3:])
                        dve.wait_ge(s_xw, m + 1)
                        nc.vector.tensor_reduce(mpart[:, i // 2, i % 2:i % 2 + 1],
                                                psX[:, (i % 2) * HALF:(i % 2 + 1) * HALF], AX.X, ALU.max)\
                            .then_inc(s_xr, 1)
                        if i == 63:
                            dve.wait_ge(s_xr, m + 1)
                            nc.vector.tensor_reduce(mcol[:, :], mpart[:, :, :], AX.X, ALU.max).then_inc(s_mcol, 1)
                    yield

            def normalise_chunk(k, n):
                s, half, i = lane_of(k), n // NT, chunks0(k) + n
                dve.wait_ge(s_used, group0[k] + n + 1)
                dve.wait_ge(s_rden, i + 1)
                if n >= 2:
                    dve.wait_ge(s_added, added0(k) + sum(1 for j in range(n - 1) if j % NT))
                elif k == 5:
                    dve.wait_ge(s_added, added0(k))
                dst = chunk[:, n % 2, :] if n % NT else U[s][:, 0, half * HALF:(half + 1) * HALF]
                nc.vector.tensor_tensor(dst, psU[:, 0, :], rden[:, n % 2, :], ALU.mult).then_inc(s_scaled, 1)

            link_n[0] = 0
            for _ in side(-1):
                pass
            dve.wait_ge(s_xr, x_index[-1, "values1"] + 1)
            dve.sem_inc(s_done["dve"], 1)
            dve.wait_ge(s_go, 1)

            with dve.Fori(0, PAIRS) as pair:
                link_n[0] = 0
                norms[0] = 0
                for k in range(PHASES):
                    l, s = k // LANES, lane_of(k)
                    stages = side(k)
                    done = 0
                    tiles = {0: 8 * NT, 1: NT, 2: 4 * NT, 3: 4 * NT}[l]
                    if k == 0:
                        next(stages)
                        done += 1
                    for n in range(tiles):
                        t = tile0[k] + n
                        slot = ring_tile[slot_of[t]]
                        if l == 0:
                            g, jt, h = n // 32, n % 32 // 4, n // 32 * 4 + n % 4
                            dve.wait_ge(s_filled, filled0(k) + n + 1)
                            nc.vector.scalar_tensor_tensor(slot, slot, kap[s][:, h:h + 1], edge[:, jt, :],
                                                           ALU.add, ALU.mult).then_inc(s_finished, 1)
                        elif l == 1:
                            if n == 0:
                                dve.wait_ge(s_rho, rho0(k) + 1)
                            dve.wait_ge(s_used, group_of[tile_before[t]] + 1)
                            link(nc.vector.tensor_scalar(slot, rho_buf[rho_at(k, 0)], wj[s][:, n, 0:1], kap[s][:, 0:1],
                                                         ALU.mult, ALU.max))
                            nc.vector.scalar_tensor_tensor(slot, absent[:, n, :], 0.0, slot,
                                                           ALU.is_equal, ALU.mult).then_inc(s_finished, 1)
                        elif l == 2:
                            dve.wait_ge(s_filled, filled0(k) + n + 1)
                            nc.vector.tensor_scalar(slot, slot, math.exp(-CLIP), math.exp(CLIP), ALU.max, ALU.min)\
                                .then_inc(s_finished, 1)
                            if n % 2 and n >= 3:
                                normalise_chunk(k, n // 2 - 1)
                        elif n % 2:
                            if n == 1 and k == 3 * LANES:
                                dve.wait_ge(s_rden, chunks0(k))
                                dve.wait_ge(s_added, added0(k))
                            if not adds_pair(k, n // 2):
                                add_tile(dve, nc.vector, 1, k, n // 2)
                        while done < due_reader(n + 1, tiles, k, "dve"):
                            next(stages)
                            done += 1
                    if l == 2:
                        normalise_chunk(k, 2 * NT - 1)
                    for _ in stages:
                        pass
                dve.wait_ge(s_xr, x_index[PHASES - 1, "values1"] + 1)
                dve.sem_inc(s_done["dve"], 1)
                dve.wait_ge(s_go, pair + 2)
            link_n[0] = 0
            norms[0] = 0
            for _ in side(PHASES):
                pass

        @block.tensor
        def _(pe):
            mm = nc.tensor.matmul

            pe.wait_ge(s_id, 3)
            pe.wait_ge(s_adjf, NT)
            for jt in range(NT):
                if jt >= 2:
                    pe.wait_ge(s_adjr, jt - 1)
                for it in range(NT):
                    ins = nc.tensor.transpose(psS[:, jt % 2, it * P:(it + 1) * P],
                                              adj_f[:, it, jt * P:(jt + 1) * P], identf[:, :])
                ins.then_inc(s_adjT, 1)
            pe.wait_ge(s_load, 16 * N_LOADS)
            for i, (n, l) in enumerate(WEIGHTS):
                if i >= 2:
                    pe.wait_ge(s_wTr, i - 1)
                nc.tensor.transpose(psX[:, (i % 2) * HALF:(i % 2) * HALF + P], raw[n, l], identf[:, :]).then_inc(s_wT, 1)
            pe.wait_ge(s_wpad, 1)
            for g in range(2):
                i = len(WEIGHTS) + g
                pe.wait_ge(s_wTr, i - 1)
                nc.tensor.transpose(psX[:, (i % 2) * HALF:(i % 2) * HALF + P],
                                    wpad[:, g, :, :].rearrange("p q r -> p (q r)"), identf[:, :]).then_inc(s_wT, 1)
            pe.wait_ge(s_wTr, len(WEIGHTS) + 2)
            pe.wait_ge(s_setup, 1)

            def side(k):
                in_epilogue = k >= 0
                for name in side_uses(k):
                    if not uses_psX(name):
                        yield
                        continue
                    m = x_index[k, name]
                    if name == "xT":
                        in_epilogue = False
                    j = epilogue_of(k) if in_epilogue else prologue_of(k)
                    l, s = j // LANES, lane_of(j)
                    turns = name.startswith("max") and name not in ("max0", "max_rows")
                    if m - turns >= 1:
                        pe.wait_ge(s_xr, m - turns)

                    if name == "den":
                        pe.wait_ge(s_evac, evac0(j + 1))
                        for t in range(NT):
                            ins = mm(psX[:, t:t + 1], U[s][:, 1, t * P:(t + 1) * P], selD[:, :],
                                     start=True, stop=True)
                    elif name == "out":
                        if l == 2:
                            pe.wait_ge(s_added, added0(j + 1))
                        if l in (0, 3):
                            pe.wait_ge(s_norm, 1 if j == PHASES - 1 else 1 + before(j + 1, (1, 0, 0, 1)))
                        for t in range(NT):
                            o = psX[:, t * P:(t + 1) * P]
                            if l == 0:
                                mm(o, U[s][:, 0, t * P:(t + 1) * P], woutp[:, 0, :], start=True, stop=False)
                                ins = mm(o, U[s][:, 1, t * P:(t + 1) * P], woutp[:, 1, :], start=False, stop=True)
                            elif l == 1:
                                ins = nc.tensor.transpose(o, U[s][:, 0, t * P:(t + 1) * P], identf[:, :])
                            else:
                                ins = mm(o, U[s][:, 0, t * P:(t + 1) * P], wt[l, "o"][:, :], start=True, stop=True)
                    elif name == "xT":
                        if l == 0:
                            pe.wait_ge(s_x_in[s], 16)
                        else:
                            pe.wait_ge(s_xn, k + 1)
                        for t in range(NT):
                            ins = nc.tensor.transpose(psX[:, t * P:(t + 1) * P], xn[s][:, t, :], identf[:, :])
                    elif name == "tops":
                        H = HEADS[l]
                        for i in range(2):
                            ins = mm(psX[0:2 * H, i * HALF:(i + 1) * HALF], wsd[l][:, :],
                                     xT[s][:, i * HALF:(i + 1) * HALF], start=True, stop=True)
                    elif name == "top_bc":
                        H = HEADS[l]
                        pe.wait_ge(s_diag, (gat_before(j) if k >= 0 else 0) + 1)
                        ins = mm(psX[:, 0:2 * H], ones[0:2 * H, :], diag[0:2 * H, 0:2 * H], start=True, stop=True)
                    elif name in ("values0", "values1"):
                        for i in range(4):
                            t = 4 * int(name[-1]) + i
                            ins = mm(psX[:, i * 2 * P:i * 2 * P + P + HEADS[l]], xT[s][:, t * P:(t + 1) * P],
                                     wcat[l][:, :], start=True, stop=True)
                    elif name in ("q", "k"):
                        for i in range(2):
                            ins = mm(psX[:, i * HALF:(i + 1) * HALF], wt[l, name][:, :],
                                     xT[s][:, i * HALF:(i + 1) * HALF], start=True, stop=True)
                    elif name == "v":
                        for t in range(NT):
                            ins = mm(psX[:, t * P:(t + 1) * P], xT[s][:, t * P:(t + 1) * P], wt[l, "v"][:, :],
                                     start=True, stop=True)
                    elif name == "max_rows":
                        pe.wait_ge(s_mcol, j - 6 + 1)
                        ins = nc.tensor.transpose(psX[0:32, 0:P], mcol[:, :], identf[:, :])
                    else:
                        i = int(name[3:])
                        if i == 0:
                            pe.wait_ge(s_stack[l, s], 24 * 16)
                        h, t, jh = i // 16, i % 16 // 2, i % 2
                        ins = mm(psX[:, jh * HALF:(jh + 1) * HALF], qs[s][0:SPLIT_ROWS, h, t * P:(t + 1) * P],
                                 ks[s][0:SPLIT_ROWS, h, jh * HALF:(jh + 1) * HALF], start=True, stop=True)
                    ins.then_inc(s_xw, 1)
                    yield

            def rho_rows(k, h):
                l, s = k // LANES, lane_of(k)
                if h == 0 and k >= 1:
                    pe.wait_ge(s_xr, x_index[k - 1, "xT"] + 1)
                if rho0(k) + h >= 2:
                    pe.wait_ge(s_rho, rho0(k) + h - (l == 0))
                for i in range(2):
                    ins = mm(psS[:, (h + l) % 2, i * HALF:(i + 1) * HALF],
                             wsd[l][:, h:h + 1].broadcast_to([P, P]), xT[s][:, i * HALF:(i + 1) * HALF],
                             start=True, stop=True)
                ins.then_inc(s_rho_ps, 1)

            for _ in side(-1):
                pass
            pe.sem_inc(s_done["pe"], 1)
            pe.wait_ge(s_go, 1)

            with pe.Fori(0, PAIRS) as pair:
                for k in range(PHASES):
                    l, s = k // LANES, lane_of(k)
                    stages = side(k)
                    done = 0
                    tiles = {0: 8 * NT, 1: NT, 2: 4 * NT, 3: 4 * NT}[l]

                    def advance(t):
                        nonlocal done
                        while done < due(t, tiles, k):
                            next(stages)
                            done += 1

                    if l == 0:
                        if k == 0:
                            for h in range(4):
                                rho_rows(k, h)
                        rho_rows(k, 4)
                        rho_rows(k, 5)
                    if k >= 1:
                        pe.wait_ge(s_evac, evac0(k))
                        pe.wait_ge(s_filled, filled0(k))
                        if l >= 1:
                            pe.wait_ge(s_rho, rho0(k))
                        if chunks0(k):
                            pe.wait_ge(s_scaled, chunks0(k))
                    if l == 0:
                        if k >= 1:
                            pe.wait_ge(s_xr, x_index[k - 1, "values1"] + 1)
                        for g in range(2):
                            if g == 1:
                                pe.wait_ge(s_evac, evac0(k) + 1)
                            for jt in range(NT):
                                if g == 0 and jt in (4, 5):
                                    rho_rows(k, 2 + jt)
                                if g == 1 and jt == 3:
                                    for h in range(2 if k + 1 < LANES else 1):
                                        rho_rows(k + 1, h)
                                if g == 1 and jt == 5 and k + 1 < LANES:
                                    rho_rows(k + 1, 2)
                                    rho_rows(k + 1, 3)
                                n = 4 * (g * NT + jt)
                                pe.wait_ge(s_finished, finished0(k) + n + 4)
                                for i in range(2):
                                    for q in range(4):
                                        t = tile0[k] + n + q
                                        ins = mm(psU[q * 32:(q + 1) * 32, i, :], vpad[s][:, jt, 4 * g + q, :],
                                                 ring_tile[slot_of[t]][:, i * HALF:(i + 1) * HALF],
                                                 start=(jt == 0), stop=(jt == NT - 1))
                                ins.then_inc(s_used, 1)
                                advance(n + 4)
                    elif l == 1:
                        if k > LANES:
                            rho_rows(k, 0)
                        pe.wait_ge(s_xr, x_index[k - 1, "values1"] + 1)
                        for jt in range(NT):
                            pe.wait_ge(s_finished, finished0(k) + jt + 1)
                            for i in range(2):
                                ins = mm(psU[:, i, :], vals[s][:, jt, :],
                                         ring_tile[slot_of[tile0[k] + jt]][:, i * HALF:(i + 1) * HALF],
                                         start=(jt == 0), stop=(jt == NT - 1))
                            if jt % 4 == 3:
                                for i in range(2):
                                    for q in range(4):
                                        j = jt - 3 + q
                                        ins = mm(psS[q * 32:(q + 1) * 32, 0, i * HALF:(i + 1) * HALF], gcol[s][:, j, :],
                                                 ring_tile[slot_of[tile0[k] + j]][:, i * HALF:(i + 1) * HALF],
                                                 start=(jt == 3), stop=(jt == NT - 1))
                                ins.then_inc(s_used, 1)
                            advance(jt + 1)
                    else:
                        rows = SPLIT_ROWS + (l == 3)
                        pe.wait_ge(s_stack[l, s], (24 + (l == 3)) * 16)
                        if l == 3:
                            pe.wait_ge(s_ones_row, s + 1)
                        pe.wait_ge(s_xr, x_index[k - 1, "v"] + 1)

                        points = POINTS[k]

                        def scores(n):
                            half, jt = n // NT, n % NT
                            cols = slice(half * HALF, (half + 1) * HALF)
                            for p in range(2):
                                if n >= 1:
                                    pe.wait_ge(s_filled, filled0(k) + 2 * (n - 1) + p + 1)
                                for i in range(2):
                                    o = psS[:, p, i * HALF:(i + 1) * HALF]
                                    h = 2 * p + i
                                    mm(o, ks[s][0:rows, h, jt * P:(jt + 1) * P], qs[s][0:rows, h, cols],
                                       start=True, stop=False)
                                    ins = mm(o, identb[:, :], absent[:, jt, cols], start=False, stop=True)
                                ins.then_inc(s_scores, 1)
                                if n >= 1 and points > 2 + p:
                                    advance(2 * n - 1.5 + p * 0.5)

                        def sums(n):
                            half, jt = n // NT, n % NT
                            if l == 2 and n >= 1:
                                pe.wait_ge(s_evac, evac0(k) + n)
                            if l == 3 and n == NT:
                                pe.wait_ge(s_evac, evac0(k) + 1)
                            if l == 2:
                                pe.wait_ge(s_finished, finished0(k) + 2 * n + 2)
                            else:
                                pe.wait_ge(s_filled, filled0(k) + 2 * n + 2)
                            for bank in (1, 0) if l == 2 else (0,):
                                if l == 2 and n >= 1 and bank == 0:
                                    pe.wait_ge(s_scaled, chunks0(k) + n)
                                for h in range(4):
                                    t = tile0[k] + 2 * n + h // 2
                                    w = ones[:, 0:HD] if bank else vals[s][:, jt, h * HD:(h + 1) * HD]
                                    ins = mm(psU[h * 32:(h + 1) * 32, bank, :], w,
                                             ring_tile[slot_of[t]][:, (h % 2) * HALF:(h % 2 + 1) * HALF],
                                             start=(l == 2 or jt == 0), stop=(l == 2 or jt == NT - 1))
                                if l == 2 and bank == 1:
                                    ins.then_inc(s_den, 1)
                                if bank == 1 and points > 1:
                                    advance(2 * n + 1.5)
                            ins.then_inc(s_used, 1)

                        def row_sums(half):
                            if half:
                                pe.wait_ge(s_evac, evac0(k) + 2)
                            for p in range(2):
                                pe.wait_ge(s_tsum[p], accumulated0(k) + (NT - 1) * (half + 1))
                            for h in range(4):
                                ins = mm(psU[h * 32:(h + 1) * 32, 1, :], ones[:, 0:HD],
                                         tile_sum[half][h // 2][:, (h % 2) * HALF:(h % 2 + 1) * HALF],
                                         start=True, stop=True)
                            ins.then_inc(s_dsum, 1)

                        scores(0)
                        for n in range(2 * NT):
                            if n + 1 < 2 * NT:
                                scores(n + 1)
                            sums(n)
                            advance(2 * n + 2)
                            if l == 3 and n == NT:
                                row_sums(0)
                        if l == 3:
                            row_sums(1)
                pe.sem_inc(s_done["pe"], 1)
                pe.wait_ge(s_go, pair + 2)
            for _ in side(PHASES):
                pass


N_LOADS = 9 + 2 * (4 + 2 + 2)

_INS = ['x', 'adj', 'L0_gnn_W', 'L0_gnn_a_src', 'L0_gnn_a_dst', 'L0_gnn_beta_tilde', 'L0_gnn_W_out', 'L1_gnn_W',
        'L1_gnn_a', 'L2_gnn_Wq', 'L2_gnn_bq', 'L2_gnn_Wk', 'L2_gnn_bk', 'L2_gnn_Wv', 'L2_gnn_bv', 'L2_gnn_Wo',
        'L2_gnn_bo', 'L2_gnn_gamma', 'L2_gnn_beta', 'L3_gnn_wq', 'L3_gnn_bq', 'L3_gnn_wk', 'L3_gnn_bk', 'L3_gnn_wv',
        'L3_gnn_bv', 'L3_gnn_wo', 'L3_gnn_bo']


def program(nc, t, out):
    build(nc, t["x"], t["adj"], t["L0_gnn_W"], t["L0_gnn_a_src"], t["L0_gnn_a_dst"], t["L0_gnn_beta_tilde"],
          t["L0_gnn_W_out"], t["L1_gnn_W"], t["L1_gnn_a"],
          {n: t[f"L2_gnn_W{n}"] for n in "qkvo"}, {n: t[f"L2_gnn_b{n}"] for n in "qkvo"},
          t["L2_gnn_gamma"], t["L2_gnn_beta"],
          {n: t[f"L3_gnn_w{n}"] for n in "qkvo"}, {n: t[f"L3_gnn_b{n}"] for n in "qkvo"}, out)


def kernel(**inputs):
    import numpy as _np
    import concourse.bacc as _bacc
    from concourse import mybir as _mybir
    from concourse.bass_utils import run_bass_kernel_spmd as _run

    nc = _bacc.Bacc("TRN2", target_bir_lowering=False, num_devices=1)
    arrays, args = {}, {}
    for name in _INS:
        a = _np.ascontiguousarray(inputs[name])
        if a.ndim == 0:
            a = a.reshape(1, 1)
        arrays[f"in_{name}_dram"] = a
        args[name] = nc.dram_tensor(f"in_{name}_dram", a.shape, _mybir.dt.from_np(a.dtype), kind="ExternalInput").ap()
    out = nc.dram_tensor("out_dram", inputs["x"].shape, _mybir.dt.float32, kind="ExternalOutput").ap()
    program(nc, args, out)
    r = _run(nc, [arrays], core_ids=[0])
    return r.results[0]["out_dram"]
```
